# Optimizing a Trainium2 kernel written in Bass

```python
import numpy as np
import jax
import jax.numpy as jnp

def _softmax(x, axis=-1):
    return jax.nn.softmax(x, axis=axis)

def _gelu(x):
    return jax.nn.gelu(x, approximate=True)

def _silu(x):
    return jax.nn.silu(x)

def _sigmoid(x):
    return jax.nn.sigmoid(x)

def _layernorm(x, axis=-1, eps=1e-05):
    m = jnp.mean(x, axis=axis, keepdims=True)
    v = jnp.var(x, axis=axis, keepdims=True)
    return (x - m) / jnp.sqrt(v + eps)

def _scatter_add(tgt, idx, src, axis=0):
    return tgt.at[idx].add(src)

def _segment_sum(src, seg, n):
    return jax.ops.segment_sum(src, seg, n)
kernel_name = 'mk_seq_preln_d1_jaxref_r8_d7b363'

def setup_inputs(seed: int=0):
    np.random.seed(seed)
    _w = jnp.asarray

    def _L0_attn_setup():
        import jax, jax.numpy as jnp
        import numpy as np
        NUM_HEADS = 16
        DIM = 128
        key = jax.random.key(seed)
        kx, kwq, kbq, kwk, kbk = jax.random.split(key, 5)
        B, N, C = (2, 256, DIM)
        s = 1.0 / np.sqrt(C)
        return {'x': jax.random.normal(kx, (B, N, C), dtype=jnp.float32), 'Wq': jax.random.normal(kwq, (C, C), dtype=jnp.float32) * s, 'bq': jax.random.normal(kbq, (C,), dtype=jnp.float32) * 0.01, 'Wk': jax.random.normal(kwk, (C, C), dtype=jnp.float32) * s, 'bk': jax.random.normal(kbk, (C,), dtype=jnp.float32) * 0.01}
    _L0_attn_in = _L0_attn_setup()

    def _L0_ffn_setup():
        import jax, jax.numpy as jnp
        import numpy as np
        D_MODEL = 128
        N_EXPERTS = 8
        TOP_K = 2
        FFN_HIDDEN = 4 * D_MODEL
        key = jax.random.key(seed)
        ks = jax.random.split(key, 6)

        def xavier(k, shape):
            fan_in, fan_out = (shape[-2], shape[-1])
            lim = jnp.sqrt(6.0 / (fan_in + fan_out))
            return jax.random.uniform(k, shape, jnp.float32, -lim, lim)
        x = jax.random.normal(ks[0], (4, 256, D_MODEL), jnp.float32)
        w_gate = xavier(ks[1], (N_EXPERTS, D_MODEL))
        W1 = xavier(ks[2], (N_EXPERTS, D_MODEL, FFN_HIDDEN))
        b1 = jnp.zeros((N_EXPERTS, FFN_HIDDEN), jnp.float32)
        W2 = xavier(ks[3], (N_EXPERTS, FFN_HIDDEN, D_MODEL))
        b2 = jnp.zeros((N_EXPERTS, D_MODEL), jnp.float32)
        return {'x': x, 'w_gate': w_gate, 'W1': W1, 'b1': b1, 'W2': W2, 'b2': b2}
    _L0_ffn_in = _L0_ffn_setup()
    _d = {'L0_attn_x': _L0_attn_in['x'], 'L0_attn_Wq': _L0_attn_in['Wq'], 'L0_attn_bq': _L0_attn_in['bq'], 'L0_attn_Wk': _L0_attn_in['Wk'], 'L0_attn_bk': _L0_attn_in['bk'], 'L0_ffn_w_gate': _L0_ffn_in['w_gate'], 'L0_ffn_W1': _L0_ffn_in['W1'], 'L0_ffn_b1': _L0_ffn_in['b1'], 'L0_ffn_W2': _L0_ffn_in['W2'], 'L0_ffn_b2': _L0_ffn_in['b2']}
    _x0 = _d['L0_attn_x']
    _d['L0_attn_x'] = jax.random.normal(jax.random.fold_in(jax.random.key(seed), 1), (4, 512, 128), dtype=_x0.dtype)
    del _x0
    return _d

def reference(L0_attn_x, L0_attn_Wq, L0_attn_bq, L0_attn_Wk, L0_attn_bk, L0_ffn_w_gate, L0_ffn_W1, L0_ffn_b1, L0_ffn_W2, L0_ffn_b2):

    def _L0_attn_ref(x, Wq, bq, Wk, bk):
        import jax, jax.numpy as jnp
        import numpy as np
        NUM_HEADS = 16
        DIM = 128
        B, N, C = x.shape
        H = NUM_HEADS
        Dh = C // H
        q = (x @ Wq + bq).reshape(B, N, H, Dh).transpose(0, 2, 1, 3)
        k = (x @ Wk + bk).reshape(B, N, H, Dh).transpose(0, 2, 1, 3)
        v = k
        scale = C ** (-0.5)
        attn = jnp.einsum('bhnd,bhmd->bhnm', q, k) * scale
        attn = jax.nn.softmax(attn, axis=-1)
        out = jnp.einsum('bhnm,bhmd->bhnd', attn, v)
        return out.transpose(0, 2, 1, 3).reshape(B, N, C)

    def _L0_ffn_ref(x, w_gate, W1, b1, W2, b2):
        import jax, jax.numpy as jnp
        import numpy as np
        D_MODEL = 128
        N_EXPERTS = 8
        TOP_K = 2
        FFN_HIDDEN = 4 * D_MODEL
        B, S, D = x.shape
        flat_x = x.reshape(-1, D)
        gate = jax.nn.softmax(flat_x @ w_gate.T, axis=-1)
        topk_scores, topk_idx = jax.lax.top_k(gate, TOP_K)
        cw = (jax.nn.one_hot(topk_idx, N_EXPERTS, dtype=flat_x.dtype) * topk_scores[..., None]).sum(axis=1)
        h = jax.nn.gelu(jnp.einsum('td,edh->teh', flat_x, W1) + b1, approximate=False)
        y = jnp.einsum('teh,ehd->ted', h, W2) + b2
        out = jnp.einsum('ted,te->td', y, cw)
        return out.reshape(B, S, D)
    x = L0_attn_x
    x = x + _L0_attn_ref(_layernorm(x, axis=-1), L0_attn_Wq, L0_attn_bq, L0_attn_Wk, L0_attn_bk)
    x = x + _L0_ffn_ref(_layernorm(x, axis=-1), L0_ffn_w_gate, L0_ffn_W1, L0_ffn_b1, L0_ffn_W2, L0_ffn_b2)
    return x

_drawn_inputs = setup_inputs


def setup_inputs(seed=0):
    import zlib

    import numpy as np

    out = dict(_drawn_inputs(seed))
    spreads = {'L0_ffn_b1': (0.0, 0.1), 'L0_ffn_b2': (0.0, 0.1)}
    factors = {'L0_attn_bq': 37.686, 'L0_attn_bk': 3.684}
    for name, (base, spread) in spreads.items():
        noise = np.random.default_rng([zlib.crc32(name.encode()), seed]).standard_normal(out[name].shape)
        drawn = base * np.exp(spread * noise) if base else spread * noise
        out[name] = jnp.asarray(drawn.astype(out[name].dtype))
    for name, factor in factors.items():
        out[name] = (out[name] * factor).astype(out[name].dtype)
    return out
```

```python
from contextlib import ExitStack

import numpy as np

import concourse.bass as bass
from concourse import mybir

ALU = mybir.AluOpType
ACT = mybir.ActivationFunctionType
AX = mybir.AxisListType
F32 = mybir.dt.float32
F16 = mybir.dt.float16
U32 = mybir.dt.uint32

P = 128
WSCALE = 64.0
EPS = 1e-5


def preln_attention_moe(nc, x, wq, bq, wk, bk, w_gate, W1, b1, W2, b2, out):
    B, N, C = x.shape
    H, Dh = 16, C // 16
    E, _, F = W1.shape
    T = N // P
    G = H // 4
    HC = F // P
    U = E * HC
    SCALE = float(C) ** -0.5
    assert C == P and Dh == 8 and N == 512

    with ExitStack() as ctx:
        def sb(name, shape, dt):
            return ctx.enter_context(nc.sbuf_tensor(name, shape, dt))

        def psum(name, shape, dt):
            return ctx.enter_context(nc.psum_tensor(name, shape, dt))

        def sem(name):
            return ctx.enter_context(nc.semaphore(name))

        ident = sb("ident", [P, P], F32)
        ident16 = sb("ident16", [P, P], F16)
        iota8 = sb("iota8", [P, E], F32)
        iota8i = sb("iota8i", [P, E], mybir.dt.int32)
        neg_half = sb("neg_half", [P, T], F32)
        pick = sb("pick", [2 * E, E, P], F16)
        wqk = sb("wqk", [P, 2 * C], F32)
        bqk = sb("bqk", [P, 2 * C], F32)
        rows = sb("rows", [P, P], F32)
        cols = sb("cols", [P, U + 2 * E], F32)
        b2s = sb("b2s", [P, E], F32)
        wf = sb("wf", [P, 2, U * P], F32)
        wh = sb("wh", [P, 2, U * P], F16)
        wl = sb("wl", [P, 2, U * P], F16)

        xt = sb("xt", [P, T, C], F32)
        stats = sb("stats", [P, 2, T, 6], F32)
        mv = sb("mv", [P, 2, T, 2], F32)
        ve = sb("ve", [P, 2, T], F32)
        rstd = sb("rstd", [P, 2, T], F32)
        xn = sb("xn", [P, 2, T, C], F32)
        xT = sb("xT", [P, N], F32)
        qkf = sb("qkf", [P, T, 2 * C], F32)
        q_aug = sb("q_aug", [P, T, H, 32], F16)
        k_aug = sb("k_aug", [P, T, H, 32], F16)
        v_aug = sb("v_aug", [P, T, H, 32], F32)
        qT0 = sb("qT0", [P, G, N], F16)
        qT1 = sb("qT1", [P, 2, N], F16)
        kT = sb("kT", [P, G, N], F16)
        kTm = sb("kTm", [P, G, 4, N], F16)
        probs = sb("probs", [P, 4, 2, N], F32)
        avs = sb("avs", [P, 2, N], F32)
        rden = sb("rden", [P, 2, T, 4], F32)
        att = sb("att", [P, T, C], F32)
        x1 = sb("x1", [P, T, C], F32)
        x2f = sb("x2f", [P, N], F32)
        x2h = sb("x2h", [P, N], F16)
        x2l = sb("x2l", [P, N], F16)
        nl1 = sb("nl1", [P, T], F32)
        lsh = sb("lsh", [P, T, E], F32)
        gexp = sb("gexp", [P, T, E], F32)
        gsum = sb("gsum", [P, T], F32)
        grec = sb("grec", [P, T], F32)
        gate = sb("gate", [P, T, E], F32)
        top = sb("top", [P, T, 8], F32)
        topi = sb("topi", [P, T, 8], U32)
        topf = sb("topf", [P, T, 2], F32)
        pickd = sb("pickd", [P, 2, T, E], F32)
        cw = sb("cw", [P, T, E], F32)
        cwhl = sb("cwhl", [P, T, 2, E], F16)
        cwT = sb("cwT", [2 * E, N], F16)
        cwb = sb("cwb", [P, E, N], F32)
        hf = sb("hf", [P, 4, N], F32)
        hh = sb("hh", [P, 4, N], F16)
        hl = sb("hl", [P, 4, N], F16)
        ytmp = sb("ytmp", [P, N], F32)
        accT = sb("accT", [P, N], F32)
        res = sb("res", [P, T, C], F32)

        SM = [psum(f"SM{i}", [P, N], F32) for i in range(2)]
        ST = psum("ST", [P, 2, 2, N], F32)
        AV = psum("AV", [P, N], F32)
        MISC = psum("MISC", [P, N], F32)
        MISC16 = MISC[:, :].bitcast(F16)
        SM16 = [s[:, :].bitcast(F16) for s in SM]
        ST16 = ST[:, :, :, :].rearrange("p a b n -> p (a b n)").bitcast(F16)

        s_const = sem("s_const")
        s_w = sem("s_w")
        s_rows = sem("s_rows")
        s_wf = sem("s_wf")
        s_rowsT = sem("s_rowsT")
        s_cols = sem("s_cols")
        s_b2s = sem("s_b2s")
        s_wfs = sem("s_wfs")
        s_wh = sem("s_wh")
        s_wl = sem("s_wl")
        x_in = sem("x_in")
        ln_ve = sem("ln_ve")
        ln_rstd = sem("ln_rstd")
        ln_done = sem("ln_done")
        xT_full = sem("xT_full")
        xT_done = sem("xT_done")
        qk_full = sem("qk_full")
        qk_done = sem("qk_done")
        aug_hi = sem("aug_hi")
        aug_lo = sem("aug_lo")
        aug_v = sem("aug_v")
        kT_full = sem("kT_full")
        kT_done = sem("kT_done")
        qT_full = sem("qT_full")
        qT_done = sem("qT_done")
        km_in = sem("km_in")
        sm_full = sem("sm_full")
        sm_max = sem("sm_max")
        qr_full = sem("qr_full")
        qr_done = sem("qr_done")
        st_full = sem("st_full")
        exp_done = sem("exp_done")
        av_step = sem("av_step")
        av_done = sem("av_done")
        ot_full = sem("ot_full")
        ot_used = sem("ot_used")
        x1_done = sem("x1_done")
        x2_full = sem("x2_full")
        x2_done = sem("x2_done")
        x2l_done = sem("x2l_done")
        lg_full = sem("lg_full")
        lg_shift = sem("lg_shift")
        gexp_done = sem("gexp_done")
        cw_done = sem("cw_done")
        cwT_full = sem("cwT_full")
        cwT_done = sem("cwT_done")
        cwb_full = sem("cwb_full")
        cwb_done = sem("cwb_done")
        up_full = sem("up_full")
        gelu_done = sem("gelu_done")
        hh_done = sem("hh_done")
        hl_done = sem("hl_done")
        down_done = sem("down_done")
        comb_done = sem("comb_done")
        acc_done = sem("acc_done")
        fT_full = sem("fT_full")
        res_done = sem("res_done")
        out_dma = sem("out_dma")
        dve_chain = sem("dve_chain")
        pool_chain = sem("pool_chain")

        LAG_ST, LAG_AV, LAG_OT = 5, 6, 8
        SLOTS = 4 * G + LAG_OT
        LAG_DN = 3
        PAIRS = G * 4 * 2

        block = ctx.enter_context(nc.Block())

        @block.sync
        def _(sp):
            sp.dma_start(wqk[:, 0:C], wq).then_inc(s_w, 16)
            sp.dma_start(wqk[:, C:2 * C], wk).then_inc(s_w, 16)
            for b in range(B):
                if b >= 1:
                    sp.wait_ge(res_done, b)
                    sp.dma_start(out[b - 1].rearrange("(t p) c -> p t c", p=P), res[:, :, :]).then_inc(out_dma, 16)
                sp.dma_start(xt[:, :, :], x[b].rearrange("(t p) c -> p t c", p=P)).then_inc(x_in, 16)
                if b == 0:
                    sp.dma_start(bqk[:, 0:C], bq.partition_broadcast(P)).then_inc(s_w, 16)
                    sp.dma_start(bqk[:, C:2 * C], bk.partition_broadcast(P)).then_inc(s_w, 16)
                    sp.dma_start(rows[0:U, :], b1.rearrange("e (c h) -> (e c) h", h=P)).then_inc(s_rows, 16)
                    sp.dma_start(rows[U:U + E, :], w_gate).then_inc(s_rows, 16)
                    sp.dma_start(rows[U + E:U + 2 * E, :], b2).then_inc(s_rows, 16)
                    sp.dma_start(wf[:, 0, :].rearrange("p (e h) -> p e h", e=E), W1.rearrange("e d h -> d e h")).then_inc(s_wf, 16)
                    sp.dma_start(wf[:, 1, :].rearrange("p (e c d) -> p e c d", e=E, c=HC),
                                 W2.rearrange("e (c p) d -> p e c d", p=P)).then_inc(s_wf, 16)
                sp.wait_ge(kT_done, 2 * (b + 1))
                for j in range(4):
                    sp.dma_start(kTm[32 * j:32 * j + 32, :, j, :], kT[32 * j:32 * j + 32, :, :]).then_inc(km_in, 16)
            sp.wait_ge(res_done, B)
            sp.dma_start(out[B - 1].rearrange("(t p) c -> p t c", p=P), res[:, :, :]).then_inc(out_dma, 16)
            sp.wait_ge(out_dma, 16 * B)

        @block.gpsimd
        def _(pool):
            chain = [0]

            def link(ins):
                chain[0] += 1
                ins.then_inc(pool_chain, 1)
                pool.wait_ge(pool_chain, chain[0])

            link(pool.memset(ident[:, :], 0.0))
            pool.memset(neg_half[:, :], -0.5).then_inc(s_const, 1)
            pool.affine_select(out=ident[:, :], in_=ident[:, :], compare_op=ALU.not_equal, fill=1.0,
                               base=0, pattern=[[-1, P]], channel_multiplier=1).then_inc(s_const, 1)
            pool.wait_ge(s_const, 2)
            pool.tensor_copy(ident16[:, :], ident[:, :]).then_inc(s_const, 1)
            pool.iota(iota8i[:, :], pattern=[[1, E]], base=0, channel_multiplier=0).then_inc(s_const, 1)
            link(pool.memset(q_aug[:, :, :, :], 0.0))
            link(pool.memset(k_aug[:, :, :, :], 0.0))
            pool.memset(k_aug[:, :, :, 24:25], 1.0).then_inc(s_const, 1)
            link(pool.memset(v_aug[:, :, :, :], 0.0))
            pool.memset(v_aug[:, :, :, 8:9], 1.0).then_inc(s_const, 1)
            pool.memset(kTm[:, :, :, :], 0.0).then_inc(s_const, 1)
            link(pool.memset(pick[:, :, :], 0.0))
            for half in range(2):
                link(pool.affine_select(out=pick[:, :, :], in_=pick[:, :, :], compare_op=ALU.not_equal, fill=1.0,
                                        base=-half * E, pattern=[[-1, E], [0, P]], channel_multiplier=1))
            for b in range(B):
                for ln in range(2):
                    pool.wait_ge(ln_ve, 2 * b + ln + 1)
                    pool.tensor_tensor(rstd[:, ln, :], ve[:, ln, :], neg_half[:, :], ALU.pow).then_inc(ln_rstd, 1)
                    if ln == 0:
                        pool.wait_ge(aug_hi, 4 * b + 1)
                        pool.tensor_tensor(k_aug[:, :, :, 16:24], qkf[:, :, C:2 * C].rearrange("p t (h d) -> p t h d", d=Dh),
                                           k_aug[:, :, :, 0:8], ALU.subtract).then_inc(aug_lo, 1)
                        pool.wait_ge(aug_hi, 4 * b + 2)
                        pool.tensor_tensor(q_aug[:, :, :, 8:16], qkf[:, :, 0:C].rearrange("p t (h d) -> p t h d", d=Dh),
                                           q_aug[:, :, :, 0:8], ALU.subtract).then_inc(aug_lo, 1)
                        if b == 0:
                            pool.wait_ge(s_wf, 32)
                            for n in range(2):
                                pool.tensor_scalar(wf[:, n, :], wf[:, n, :], WSCALE, None, ALU.mult).then_inc(s_wfs, 1)
                            for n in range(2):
                                pool.wait_ge(s_wfs, n + 1)
                                pool.wait_ge(s_wh, n + 1)
                                pool.tensor_tensor(wl[:, n, :], wf[:, n, :], wh[:, n, :], ALU.subtract).then_inc(s_wl, 1)
                for u in range(U):
                    v = b * U + u
                    pool.wait_ge(gelu_done, v + 1)
                    pool.wait_ge(hh_done, v + 1)
                    if v >= 4:
                        pool.wait_ge(down_done, v - 3)
                    pool.tensor_tensor(hl[:, u % 4, :], hf[:, u % 4, :], hh[:, u % 4, :], ALU.subtract).then_inc(hl_done, 1)

        @block.scalar
        def _(act):
            act.wait_ge(s_rowsT, 1)
            act.activation(cols[:, :], MISC[:, 0:U + 2 * E], ACT.Copy).then_inc(s_cols, 1)
            for b in range(B):
                act.wait_ge(xT_full, b + 1)
                act.activation(xT[:, :], MISC[:, :], ACT.Copy).then_inc(xT_done, 1)
                act.wait_ge(qk_done, 2 * (b + 1))
                if b == 0:
                    act.wait_ge(s_const, 7)
                qv = qkf[:, :, 0:C].rearrange("p t (h d) -> p t h d", d=Dh)
                kv = qkf[:, :, C:2 * C].rearrange("p t (h d) -> p t h d", d=Dh)
                act.activation(k_aug[:, :, :, 0:8], kv, ACT.Copy).then_inc(aug_hi, 1)
                act.activation(q_aug[:, :, :, 0:8], qv, ACT.Copy).then_inc(aug_hi, 1)
                act.activation(k_aug[:, :, :, 8:16], kv, ACT.Copy).then_inc(aug_hi, 1)
                act.activation(q_aug[:, :, :, 16:24], qv, ACT.Copy).then_inc(aug_hi, 1)
                act.activation(v_aug[:, :, :, 0:8], kv, ACT.Copy).then_inc(aug_v, 1)
                for n in range(2):
                    act.wait_ge(kT_full, 2 * b + n + 1)
                    act.activation(kT[:, 2 * n:2 * n + 2, :].rearrange("p g n -> p (g n)"),
                                   ST16[:, 1024 * n:1024 * n + 1024], ACT.Copy).then_inc(kT_done, 1)
                if b == 0:
                    for n in range(2):
                        act.wait_ge(s_wfs, n + 1)
                        act.activation(wh[:, n, :], wf[:, n, :], ACT.Copy).then_inc(s_wh, 1)
                for s in range(SLOTS):
                    i = s - LAG_ST
                    if s % 4 == 0 and 1 <= s // 4 <= G:
                        g = s // 4 - 1
                        act.wait_ge(qr_full, G * b + g + 1)
                        act.activation(qT1[:, g % 2, :], MISC16[:, 0:N], ACT.Copy).then_inc(qr_done, 1)
                    if 0 <= i < 4 * G:
                        for pr in range(2):
                            n = PAIRS * b + 2 * i + pr
                            act.wait_ge(st_full, n + 1)
                            if n >= 4:
                                act.wait_ge(av_step, (n - 4) // 2 + 1)
                            act.activation(probs[:, n % 4, :, :], ST[:, n % 2, :, :], ACT.Exp, scale=SCALE).then_inc(exp_done, 1)
                    k = s - LAG_AV
                    if k >= 0 and k % 4 == 3 and k // 4 < G:
                        g = k // 4
                        act.wait_ge(av_step, 4 * (G * b + g + 1))
                        act.activation(avs[:, g % 2, :], AV[:, :], ACT.Copy).then_inc(av_done, 1)
                act.wait_ge(x2_full, b + 1)
                act.activation(x2h[:, :], MISC[:, :], ACT.Copy).then_inc(x2_done, 1)
                act.activation(x2f[:, :], MISC[:, :], ACT.Copy).then_inc(x2_done, 1)
                act.wait_ge(lg_shift, b + 1)
                act.activation(gexp[:, :, :], lsh[:, :, :], ACT.Exp).then_inc(gexp_done, 1)
                for u in range(U):
                    v = b * U + u
                    act.wait_ge(up_full, v + 1)
                    if v >= 4:
                        act.wait_ge(hl_done, v - 3)
                    act.activation(hf[:, u % 4, :], ST[:, (u // 2) % 2, u % 2, :], ACT.Gelu, bias=cols[:, u:u + 1],
                                   scale=1.0 / WSCALE).then_inc(gelu_done, 1)
                    e = u - 5
                    if 0 <= e < E:
                        act.wait_ge(cwb_full, E * b + e + 1)
                        if e == 0 and b >= 1:
                            act.wait_ge(comb_done, E * b)
                        act.activation(cwb[:, e, :], MISC[:, :], ACT.Copy, scale=1.0 / WSCALE).then_inc(cwb_done, 1)

        @block.vector
        def _(dve):
            chain = [0]

            def link(ins):
                chain[0] += 1
                ins.then_inc(dve_chain, 1)
                dve.wait_ge(dve_chain, chain[0])

            def layernorm(b, ln, src):
                for t in range(T):
                    last = dve.bn_stats(stats[:, ln, t, :], src[:, t, :])
                link(last)
                for t in range(T):
                    last = dve.bn_aggr(mv[:, ln, t, :], stats[:, ln, t, :])
                link(last)
                dve.tensor_scalar(ve[:, ln, :], mv[:, ln, :, 1], EPS, None, ALU.add).then_inc(ln_ve, 1)
                dve.wait_ge(ln_rstd, 2 * b + ln + 1)
                for t in range(T):
                    dve.tensor_scalar(xn[:, ln, t, :], src[:, t, :], mv[:, ln, t, 0:1], rstd[:, ln, t:t + 1],
                                      ALU.subtract, ALU.mult).then_inc(ln_done, 1)

            for b in range(B):
                dve.wait_ge(x_in, 16 * (b + 1))
                layernorm(b, 0, xt)
                if b == 0:
                    dve.wait_ge(s_w, 64)
                for n in range(2):
                    dve.wait_ge(qk_full, 2 * b + n + 1)
                    dve.tensor_tensor(qkf[:, 2 * n:2 * n + 2, :], SM[n][:, :].rearrange("p (t c) -> p t c", t=2),
                                      bqk[:, :].unsqueeze(1).broadcast_to([P, 2, 2 * C]), ALU.add).then_inc(qk_done, 1)
                if b == 0:
                    dve.wait_ge(s_const, 4)
                    dve.tensor_copy(iota8[:, :], iota8i[:, :]).then_inc(s_b2s, 1)
                    dve.wait_ge(s_cols, 1)
                    dve.tensor_scalar(b2s[:, :], cols[:, U + E:U + 2 * E], WSCALE, None, ALU.mult).then_inc(s_b2s, 1)
                for n in range(2):
                    dve.wait_ge(qT_full, 2 * b + n + 1)
                    dve.tensor_copy(qT0[:, 2 * n:2 * n + 2, :].rearrange("p g n -> p (g n)"), SM16[n]).then_inc(qT_done, 1)
                for s in range(SLOTS):
                    if s < 4 * G:
                        for qc in range(T):
                            n = 4 * s + qc
                            dve.wait_ge(sm_full, 16 * G * b + n + 1)
                            dve.tensor_reduce(q_aug[:, qc, s, 24:25], SM[n % 2][:, :], AX.X, ALU.max,
                                              negate=True).then_inc(sm_max, 1)
                    k = s - LAG_OT
                    if k >= 0 and k % 4 == 3:
                        g = k // 4
                        dve.wait_ge(ot_full, G * b + g + 1)
                        ot = MISC[:, :].rearrange("p (t j r) -> p t j r", t=T, r=32)
                        link(dve.reciprocal(rden[:, g % 2, :, :], ot[:, :, :, 8]))
                        dve.tensor_tensor(att[:, :, 32 * g:32 * g + 32].rearrange("p t (j d) -> p t j d", d=Dh),
                                          ot[:, :, :, 0:8],
                                          rden[:, g % 2, :, :].unsqueeze(3).broadcast_to([P, T, 4, Dh]),
                                          ALU.mult).then_inc(ot_used, 1)
                dve.wait_ge(ot_used, G * (b + 1))
                dve.tensor_tensor(x1[:, :, :], xt[:, :, :], att[:, :, :], ALU.add).then_inc(x1_done, 1)
                dve.wait_ge(x1_done, b + 1)
                layernorm(b, 1, x1)
                dve.wait_ge(x2_done, 2 * (b + 1))
                dve.tensor_tensor(x2l[:, :], x2f[:, :], x2h[:, :], ALU.subtract).then_inc(x2l_done, 1)
                dve.wait_ge(lg_full, b + 1)
                lg = SM[0][:, 0:T * E].rearrange("p (t e) -> p t e", e=E)

                def per_tile(a):
                    return a.unsqueeze(2).broadcast_to([P, T, E])

                link(dve.tensor_reduce(nl1[:, :], lg, AX.X, ALU.max))
                dve.tensor_tensor(lsh[:, :, :], lg, per_tile(nl1[:, :]), ALU.subtract).then_inc(lg_shift, 1)
                dve.wait_ge(gexp_done, b + 1)
                link(dve.tensor_reduce(gsum[:, :], gexp[:, :, :], AX.X, ALU.add))
                link(dve.reciprocal(grec[:, :], gsum[:, :]))
                link(dve.tensor_tensor(gate[:, :, :], gexp[:, :, :], per_tile(grec[:, :]), ALU.mult))
                for t in range(T):
                    last = dve.max(top[:, t, :], gate[:, t, :])
                link(last)
                for t in range(T):
                    last = dve.max_index(topi[:, t, :], top[:, t, :], gate[:, t, :])
                link(last)
                link(dve.tensor_copy(topf[:, :, :], topi[:, :, 0:2]))
                for r in range(2):
                    last = dve.tensor_tensor(pickd[:, r, :, :], iota8[:, :].unsqueeze(1).broadcast_to([P, T, E]),
                                             per_tile(topf[:, :, r]), ALU.is_equal)
                link(last)
                link(dve.tensor_tensor(pickd[:, 0, :, :], pickd[:, 0, :, :], pickd[:, 1, :, :], ALU.add))
                link(dve.tensor_tensor(cw[:, :, :], gate[:, :, :], pickd[:, 0, :, :], ALU.mult))
                link(dve.tensor_copy(cwhl[:, :, 0, :], cw[:, :, :]))
                dve.tensor_tensor(cwhl[:, :, 1, :], cw[:, :, :], cwhl[:, :, 0, :], ALU.subtract).then_inc(cw_done, 1)
                for u in range(U + LAG_DN + 1):
                    if u < U:
                        v = b * U + u
                        dve.wait_ge(gelu_done, v + 1)
                        if v >= 4:
                            dve.wait_ge(down_done, v - 3)
                        dve.tensor_copy(hh[:, u % 4, :], hf[:, u % 4, :]).then_inc(hh_done, 1)
                    if u == 2:
                        dve.wait_ge(cwT_full, b + 1)
                        dve.tensor_copy(cwT[:, :], MISC16[0:2 * E, 0:N]).then_inc(cwT_done, 1)
                    w = u - LAG_DN - 1
                    if w >= 0 and w % HC == HC - 1:
                        e = w // HC
                        dve.wait_ge(down_done, b * U + w + 1)
                        dve.wait_ge(cwb_done, E * b + e + 1)
                        if b + e == 0:
                            dve.wait_ge(s_b2s, 2)
                        dst = accT if e == 0 else ytmp
                        if e == 0 and b >= 1:
                            dve.wait_ge(fT_full, b)
                        if e >= 2:
                            dve.wait_ge(acc_done, (E - 1) * b + e - 1)
                        dve.scalar_tensor_tensor(out=dst[:, :], in0=SM[e % 2][:, :], scalar=b2s[:, e:e + 1],
                                                 in1=cwb[:, e, :], op0=ALU.add, op1=ALU.mult).then_inc(comb_done, 1)
                        if e >= 1:
                            dve.wait_ge(comb_done, E * b + e + 1)
                            dve.tensor_tensor(accT[:, :], accT[:, :], ytmp[:, :], ALU.add).then_inc(acc_done, 1)
                dve.wait_ge(fT_full, b + 1)
                if b >= 1:
                    dve.wait_ge(out_dma, 16 * b)
                dve.tensor_tensor(res[:, :, :], x1[:, :, :], AV[:, :].rearrange("p (t c) -> p t c", t=T),
                                  ALU.add).then_inc(res_done, 1)

        @block.tensor
        def _(pe):
            pe.wait_ge(s_const, 3)
            pe.wait_ge(s_rows, 48)
            pe.transpose(MISC[:, 0:U + 2 * E], rows[0:U + 2 * E, :], ident[0:U + 2 * E, 0:U + 2 * E]).then_inc(s_rowsT, 1)
            pe.wait_ge(s_cols, 1)
            for b in range(B):
                for t in range(T):
                    pe.wait_ge(ln_done, 2 * T * b + t + 1)
                    last = pe.transpose(MISC[:, P * t:P * t + P], xn[:, 0, t, :], ident[:, :])
                last.then_inc(xT_full, 1)
                pe.wait_ge(xT_done, b + 1)
                if b == 0:
                    pe.wait_ge(s_w, 64)
                for t in range(T):
                    last = pe.matmul(SM[t // 2][:, 256 * (t % 2):256 * (t % 2) + 256], xT[:, P * t:P * t + P],
                                     wqk[:, :], start=True, stop=True)
                    if t % 2:
                        last.then_inc(qk_full, 1)
                pe.wait_ge(aug_hi, 4 * (b + 1))
                pe.wait_ge(aug_lo, 2 * b + 1)
                for g in range(G):
                    for t in range(T):
                        last = pe.transpose(ST16[:, N * g + P * t:N * g + P * t + P],
                                            k_aug[:, t, 4 * g:4 * g + 4, :].rearrange("p h r -> p (h r)"), ident16[:, :])
                    if g % 2:
                        last.then_inc(kT_full, 1)
                pe.wait_ge(aug_lo, 2 * b + 2)
                for g in range(G):
                    for t in range(T):
                        last = pe.transpose(SM16[g // 2][:, N * (g % 2) + P * t:N * (g % 2) + P * t + P],
                                            q_aug[:, t, 4 * g:4 * g + 4, :].rearrange("p h r -> p (h r)"), ident16[:, :])
                    if g % 2:
                        last.then_inc(qT_full, 1)
                pe.wait_ge(qT_done, 2 * (b + 1))
                pe.wait_ge(km_in, 64 * (b + 1))
                for s in range(SLOTS):
                    i = s - LAG_ST
                    for k in range(4):
                        if s < 4 * G:
                            n = 4 * s + k
                            if n >= 2:
                                pe.wait_ge(sm_max, 16 * G * b + n - 1)
                            pe.matmul(SM[n % 2][:, :], qT0[:, s // 4, P * k:P * k + P], kTm[:, s // 4, s % 4, :],
                                      start=True, stop=True).then_inc(sm_full, 1)
                        if 0 <= i < 4 * G:
                            g, c = i // 4, i % 4
                            n = PAIRS * b + 2 * i + k // 2
                            if k % 2 == 0:
                                if n >= 2:
                                    pe.wait_ge(exp_done, n - 1)
                                if c == 0:
                                    pe.wait_ge(qr_done, G * b + g + 1)
                            mm = pe.matmul(ST[:, n % 2, k % 2, :], kTm[:, g, k, P * c:P * c + P], qT1[:, g % 2, :],
                                           start=True, stop=True)
                            if k % 2:
                                mm.then_inc(st_full, 1)
                    if s % 4 == 0 and 1 <= s // 4 <= G:
                        g = s // 4 - 1
                        pe.wait_ge(sm_max, 16 * (G * b + g + 1))
                        if g >= 2:
                            pe.wait_ge(ot_used, G * b + g - 1)
                        for t in range(T):
                            last = pe.transpose(MISC16[:, P * t:P * t + P],
                                                q_aug[:, t, 4 * g:4 * g + 4, :].rearrange("p h r -> p (h r)"), ident16[:, :])
                        last.then_inc(qr_full, 1)
                    k = s - LAG_AV
                    if 0 <= k < 4 * G:
                        g, c = k // 4, k % 4
                        if c == 0 and G * b + g >= 1:
                            pe.wait_ge(av_done, G * b + g)
                        for j in range(4):
                            pe.wait_ge(exp_done, PAIRS * b + 2 * k + j // 2 + 1)
                            last = pe.matmul(AV[32 * j:32 * j + 32, :], v_aug[:, c, 4 * g + j, :],
                                             probs[:, (2 * k + j // 2) % 4, j % 2, :], start=(c == 0), stop=(c == T - 1))
                        last.then_inc(av_step, 1)
                    k = s - LAG_OT
                    if k >= 0 and k % 4 == 3:
                        g = k // 4
                        pe.wait_ge(av_done, G * b + g + 1)
                        if g >= 1:
                            pe.wait_ge(ot_used, G * b + g)
                        for t in range(T):
                            last = pe.transpose(MISC[:, P * t:P * t + P], avs[:, g % 2, P * t:P * t + P], ident[:, :])
                        last.then_inc(ot_full, 1)
                for t in range(T):
                    pe.wait_ge(ln_done, 2 * T * b + T + t + 1)
                    last = pe.transpose(MISC[:, P * t:P * t + P], xn[:, 1, t, :], ident[:, :])
                last.then_inc(x2_full, 1)
                pe.wait_ge(x2_done, 2 * (b + 1))
                for t in range(T):
                    last = pe.matmul(SM[0][:, E * t:E * t + E], x2f[:, P * t:P * t + P], cols[:, U:U + E],
                                     start=True, stop=True)
                last.then_inc(lg_full, 1)
                if b == 0:
                    pe.wait_ge(s_wl, 2)
                for u in range(U + LAG_DN):
                    if u < U:
                        v = b * U + u
                        up = ST[:, (u // 2) % 2, u % 2, :]
                        if u >= 4:
                            pe.wait_ge(gelu_done, v - 3)
                        w = slice(P * u, P * u + P)
                        pe.matmul(up, wh[:, 0, w], x2h[:, :], start=True, stop=False)
                        if u == 0:
                            pe.wait_ge(x2l_done, b + 1)
                        pe.matmul(up, wh[:, 0, w], x2l[:, :], start=False, stop=False)
                        pe.matmul(up, wl[:, 0, w], x2h[:, :], start=False, stop=True).then_inc(up_full, 1)
                    if u == 2:
                        pe.wait_ge(cw_done, b + 1)
                        for t in range(T):
                            last = pe.transpose(MISC16[0:2 * E, P * t:P * t + P],
                                                cwhl[:, t, :, :].rearrange("p a e -> p (a e)"), ident16[:, :])
                        last.then_inc(cwT_full, 1)
                    e = u - 4
                    if 0 <= e < E:
                        if e == 0:
                            pe.wait_ge(cwT_done, b + 1)
                        else:
                            pe.wait_ge(cwb_done, E * b + e)
                        pe.matmul(MISC[:, :], pick[:, e, :], cwT[:, :], start=True, stop=True).then_inc(cwb_full, 1)
                    w = u - LAG_DN
                    if w >= 0:
                        e, c = w // HC, w % HC
                        v = b * U + w
                        y = SM[e % 2][:, :]
                        pe.wait_ge(hh_done, v + 1)
                        if c == 0 and e >= 2:
                            pe.wait_ge(comb_done, E * b + e - 1)
                        ws = slice(P * w, P * w + P)
                        pe.matmul(y, wh[:, 1, ws], hh[:, w % 4, :], start=(c == 0), stop=False)
                        pe.matmul(y, wl[:, 1, ws], hh[:, w % 4, :], start=False, stop=False)
                        pe.wait_ge(hl_done, v + 1)
                        pe.matmul(y, wh[:, 1, ws], hl[:, w % 4, :], start=False, stop=(c == HC - 1)).then_inc(down_done, 1)
                pe.wait_ge(acc_done, (E - 1) * (b + 1))
                for t in range(T):
                    last = pe.transpose(AV[:, P * t:P * t + P], accT[:, P * t:P * t + P], ident[:, :])
                last.then_inc(fT_full, 1)
                pe.wait_ge(res_done, b + 1)


_INS = ["L0_attn_x", "L0_attn_Wq", "L0_attn_bq", "L0_attn_Wk", "L0_attn_bk",
        "L0_ffn_w_gate", "L0_ffn_W1", "L0_ffn_b1", "L0_ffn_W2", "L0_ffn_b2"]


def kernel(**inputs):
    import concourse.bacc as bacc
    from concourse.bass_utils import run_bass_kernel_spmd

    nc = bacc.Bacc("TRN2", target_bir_lowering=False, num_devices=1)
    arrays, args = {}, []
    for name in _INS:
        a = np.ascontiguousarray(inputs[name])
        arrays[name] = a
        args.append(nc.dram_tensor(name, a.shape, mybir.dt.from_np(a.dtype), kind="ExternalInput").ap())
    args.append(nc.dram_tensor("out", inputs["L0_attn_x"].shape, F32, kind="ExternalOutput").ap())
    preln_attention_moe(nc, *args)
    r = run_bass_kernel_spmd(nc, [arrays], core_ids=[0])
    return r.results[0]["out"]
```

```python
from contextlib import ExitStack

import numpy as np

import concourse.bass as bass
from concourse import mybir

ALU = mybir.AluOpType
ACT = mybir.ActivationFunctionType
AX = mybir.AxisListType
F32 = mybir.dt.float32
F16 = mybir.dt.float16
U32 = mybir.dt.uint32

P = 128
WSCALE = 64.0
EPS = 1e-5


def preln_attention_moe(nc, x, wq, bq, wk, bk, w_gate, W1, b1, W2, b2, out):
    B, N, C = x.shape
    H, Dh = 16, C // 16
    E, _, F = W1.shape
    T = N // P
    G = H // 4
    HC = F // P
    RING = 8
    U = E * HC
    SCALE = float(C) ** -0.5
    assert C == P and Dh == 8 and N == 512

    with ExitStack() as ctx:
        def sb(name, shape, dt):
            return ctx.enter_context(nc.sbuf_tensor(name, shape, dt))

        def psum(name, shape, dt):
            return ctx.enter_context(nc.psum_tensor(name, shape, dt))

        def sem(name):
            return ctx.enter_context(nc.semaphore(name))

        ident = sb("ident", [P, P], F32)
        ident16 = sb("ident16", [P, P], F16)
        iota8 = sb("iota8", [P, E], F32)
        iota8i = sb("iota8i", [P, E], mybir.dt.int32)
        neg_half = sb("neg_half", [P, T], F32)
        pick = sb("pick", [2 * E, E, P], F16)
        wqk = sb("wqk", [P, 2 * C], F32)
        bqk = sb("bqk", [P, 2 * C], F32)
        rows = sb("rows", [P, P], F32)
        cols = sb("cols", [P, U + 2 * E], F32)
        b2s = sb("b2s", [P, E], F32)
        wf = sb("wf", [P, 2, U * P], F32)
        wh = sb("wh", [P, 2, U * P], F16)
        wl = sb("wl", [P, 2, U * P], F16)

        xt = sb("xt", [P, T, C], F32)
        stats = sb("stats", [P, 2, T, 6], F32)
        mv = sb("mv", [P, 2, T, 2], F32)
        ve = sb("ve", [P, 2, T], F32)
        rstd = sb("rstd", [P, 2, T], F32)
        xn = sb("xn", [P, 2, T, C], F32)
        xT = sb("xT", [P, N], F32)
        qkf = sb("qkf", [P, T, 2 * C], F32)
        q_aug = sb("q_aug", [P, T, H, 32], F16)
        k_aug = sb("k_aug", [P, T, H, 32], F16)
        v_aug = sb("v_aug", [P, T, H, 32], F32)
        qT0 = sb("qT0", [P, G, N], F16)
        qT1 = sb("qT1", [P, 2, N], F16)
        kT = sb("kT", [P, G, N], F16)
        kTm = sb("kTm", [P, G, 4, N], F16)
        probs = sb("probs", [P, 4, 2, N], F32)
        avs = sb("avs", [P, 2, N], F32)
        rden = sb("rden", [P, 2, T, 4], F32)
        att = sb("att", [P, T, C], F32)
        x1 = sb("x1", [P, T, C], F32)
        x2f = sb("x2f", [P, N], F32)
        x2h = sb("x2h", [P, N], F16)
        x2l = sb("x2l", [P, N], F16)
        nl1 = sb("nl1", [P, T], F32)
        lsh = sb("lsh", [P, T, E], F32)
        gexp = sb("gexp", [P, T, E], F32)
        gsum = sb("gsum", [P, T], F32)
        grec = sb("grec", [P, T], F32)
        gate = sb("gate", [P, T, E], F32)
        top = sb("top", [P, T, 8], F32)
        topi = sb("topi", [P, T, 8], U32)
        topf = sb("topf", [P, T, 2], F32)
        pickd = sb("pickd", [P, 2, T, E], F32)
        cw = sb("cw", [P, T, E], F32)
        cwhl = sb("cwhl", [P, T, 2, E], F16)
        cwT = sb("cwT", [2 * E, N], F16)
        hf = sb("hf", [P, 4, N], F32)
        hh = sb("hh", [P, RING, N], F16)
        hl = sb("hl", [P, RING, N], F16)
        ytmp = sb("ytmp", [P, N], F32)
        accT = sb("accT", [P, N], F32)
        res = sb("res", [P, T, C], F32)

        cwb = wf[:, 0, :].rearrange("p (e n) -> p e n", e=E)

        SM = [psum(f"SM{i}", [P, N], F32) for i in range(2)]
        ST = psum("ST", [P, 2, 2, N], F32)
        AV = psum("AV", [P, N], F32)
        MISC = psum("MISC", [P, N], F32)
        MISC16 = MISC[:, :].bitcast(F16)
        SM16 = [s[:, :].bitcast(F16) for s in SM]
        UP = [ST[:, 0, i, :] for i in range(2)]
        Y = [ST[:, 1, i, :] for i in range(2)]

        s_const = sem("s_const")
        s_w = sem("s_w")
        s_rows = sem("s_rows")
        s_wf = [sem("s_w1"), sem("s_w2")]
        s_rowsT = sem("s_rowsT")
        s_cols = sem("s_cols")
        s_b2s = sem("s_b2s")
        s_wfs = sem("s_wfs")
        s_wh = sem("s_wh")
        s_wl = sem("s_wl")
        x_in = sem("x_in")
        ln_ve = sem("ln_ve")
        ln_rstd = sem("ln_rstd")
        ln_done = [sem("ln1_done"), sem("ln2_done")]
        xT_full = sem("xT_full")
        xT_done = sem("xT_done")
        qk_full = sem("qk_full")
        qk_done = sem("qk_done")
        aug_hi = sem("aug_hi")
        aug_lo = sem("aug_lo")
        s_aug0 = sem("s_aug0")
        s_kTm = sem("s_kTm")
        kT_full = sem("kT_full")
        kT_done = sem("kT_done")
        qT_full = sem("qT_full")
        qT_done = sem("qT_done")
        km_in = sem("km_in")
        sm_full = sem("sm_full")
        sm_max = sem("sm_max")
        qr_full = sem("qr_full")
        qr_done = sem("qr_done")
        st_full = sem("st_full")
        exp_done = sem("exp_done")
        av_step = sem("av_step")
        av_done = sem("av_done")
        ot_full = sem("ot_full")
        ot_used = sem("ot_used")
        x1_done = sem("x1_done")
        x2_full = sem("x2_full")
        x2_done = sem("x2_done")
        x2l_done = sem("x2l_done")
        lg_full = sem("lg_full")
        lg_shift = sem("lg_shift")
        gexp_done = sem("gexp_done")
        cw_done = sem("cw_done")
        cwT_full = sem("cwT_full")
        cwT_done = sem("cwT_done")
        cwb_full = sem("cwb_full")
        cwb_done = sem("cwb_done")
        up_full = sem("up_full")
        gelu_done = sem("gelu_done")
        hh_done = sem("hh_done")
        hl_done = sem("hl_done")
        down_done = sem("down_done")
        comb_done = sem("comb_done")
        acc_done = sem("acc_done")
        fT_full = sem("fT_full")
        res_done = sem("res_done")
        out_dma = sem("out_dma")
        dve_chain = sem("dve_chain")
        pool_chain = sem("pool_chain")

        LEAD = 20
        SLOTS = 4 * G + 2
        SM_N = 4 * H
        PAIRS = G * 4 * 2
        LAG_DN = 5
        UNITS = U + LAG_DN + 1

        def ot_slot(g):
            return 4 * g + 6 if g < G - 1 else SLOTS - 1

        block = ctx.enter_context(nc.Block())

        @block.sync
        def _(sp):
            sp.dma_start(xt[:, :, :], x[0].rearrange("(t p) c -> p t c", p=P)).then_inc(x_in, 16)
            sp.dma_start(wqk[:, 0:C], wq).then_inc(s_w, 16)
            sp.dma_start(wqk[:, C:2 * C], wk).then_inc(s_w, 16)
            sp.dma_start(bqk[:, 0:C], bq.partition_broadcast(P)).then_inc(s_w, 16)
            sp.dma_start(bqk[:, C:2 * C], bk.partition_broadcast(P)).then_inc(s_w, 16)
            sp.dma_start(wf[:, 0, :].rearrange("p (e h) -> p e h", e=E), W1.rearrange("e d h -> d e h")).then_inc(s_wf[0], 16)
            sp.dma_start(rows[0:U, :], b1.rearrange("e (c h) -> (e c) h", h=P)).then_inc(s_rows, 16)
            sp.dma_start(rows[U:U + E, :], w_gate).then_inc(s_rows, 16)
            sp.dma_start(rows[U + E:U + 2 * E, :], b2).then_inc(s_rows, 16)
            sp.dma_start(wf[:, 1, :].rearrange("p (e c d) -> p e c d", e=E, c=HC),
                         W2.rearrange("e (c p) d -> p e c d", p=P)).then_inc(s_wf[1], 16)
            for b in range(B):
                if b == 0:
                    sp.wait_ge(s_kTm, 1)
                sp.wait_ge(kT_done, 2 * (b + 1))
                for j in range(4):
                    sp.dma_start(kTm[32 * j:32 * j + 32, :, j, :], kT[32 * j:32 * j + 32, :, :]).then_inc(km_in, 16)
                if b >= 1:
                    sp.wait_ge(res_done, b)
                    sp.dma_start(out[b - 1].rearrange("(t p) c -> p t c", p=P), res[:, :, :]).then_inc(out_dma, 16)
                if b + 1 < B:
                    sp.wait_ge(x1_done, G * (b + 1))
                    sp.dma_start(xt[:, :, :], x[b + 1].rearrange("(t p) c -> p t c", p=P)).then_inc(x_in, 16)
            sp.wait_ge(res_done, B)
            sp.dma_start(out[B - 1].rearrange("(t p) c -> p t c", p=P), res[:, :, :]).then_inc(out_dma, 16)
            sp.wait_ge(out_dma, 16 * B)

        @block.gpsimd
        def _(pool):
            chain = [0]

            def link(ins):
                chain[0] += 1
                ins.then_inc(pool_chain, 1)
                pool.wait_ge(pool_chain, chain[0])

            def inv_sqrt(b, ln):
                pool.wait_ge(ln_ve, 2 * b + ln + 1)
                pool.tensor_tensor(rstd[:, ln, :], ve[:, ln, :], neg_half[:, :], ALU.pow).then_inc(ln_rstd, 1)

            link(pool.memset(ident[:, :], 0.0))
            pool.memset(neg_half[:, :], -0.5).then_inc(s_const, 1)
            pool.affine_select(out=ident[:, :], in_=ident[:, :], compare_op=ALU.not_equal, fill=1.0,
                               base=0, pattern=[[-1, P]], channel_multiplier=1).then_inc(s_const, 1)
            pool.wait_ge(s_const, 2)
            pool.tensor_copy(ident16[:, :], ident[:, :]).then_inc(s_const, 1)
            inv_sqrt(0, 0)
            pool.memset(kTm[:, :, :, :], 0.0).then_inc(s_kTm, 1)
            pool.iota(iota8i[:, :], pattern=[[1, E]], base=0, channel_multiplier=0).then_inc(s_const, 1)
            link(pool.memset(pick[:, :, :], 0.0))
            for half in range(2):
                link(pool.affine_select(out=pick[:, :, :], in_=pick[:, :, :], compare_op=ALU.not_equal, fill=1.0,
                                        base=-half * E, pattern=[[-1, E], [0, P]], channel_multiplier=1))
            for n in range(2):
                pool.wait_ge(s_wh, n + 1)
                pool.tensor_tensor(wl[:, n, :], wf[:, n, :], wh[:, n, :], ALU.subtract).then_inc(s_wl, 1)
            for b in range(B):
                inv_sqrt(b, 1)
                for u in range(U):
                    v = b * U + u
                    pool.wait_ge(gelu_done, v + 1)
                    pool.wait_ge(hh_done, v + 1)
                    if v >= RING:
                        pool.wait_ge(down_done, v - RING + 1)
                    pool.tensor_tensor(hl[:, u % RING, :], hf[:, u % 4, :], hh[:, u % RING, :],
                                       ALU.subtract).then_inc(hl_done, 1)
                    if u == 6 and b + 1 < B:
                        inv_sqrt(b + 1, 0)

        @block.scalar
        def _(act):
            qv = qkf[:, :, 0:C].rearrange("p t (h d) -> p t h d", d=Dh)
            kv = qkf[:, :, C:2 * C].rearrange("p t (h d) -> p t h d", d=Dh)

            def take_xT(b):
                act.wait_ge(xT_full, b + 1)
                act.activation(xT[:, :], SM[0][:, :], ACT.Copy).then_inc(xT_done, 1)

            def hi_part(b, n):
                act.wait_ge(qk_done, 2 * (b + 1))
                if b == 0:
                    act.wait_ge(s_aug0, 3)
                dst, src = [(k_aug[:, :, :, 0:8], kv), (k_aug[:, :, :, 8:16], kv), (q_aug[:, :, :, 0:8], qv),
                            (q_aug[:, :, :, 16:24], qv), (v_aug[:, :, :, 0:8], kv)][n]
                act.activation(dst, src, ACT.Copy).then_inc(aug_hi, 1)

            def take_kT(b, n):
                act.wait_ge(kT_full, 2 * b + n + 1)
                act.activation(kT[:, 2 * n:2 * n + 2, :].rearrange("p g n -> p (g n)"), SM16[n],
                               ACT.Copy).then_inc(kT_done, 1)

            def take_qr(b, g):
                act.wait_ge(qr_full, G * b + g + 1)
                act.activation(qT1[:, g % 2, :], MISC16[:, 0:N], ACT.Copy).then_inc(qr_done, 1)

            take_xT(0)
            for n in range(5):
                hi_part(0, n)
            for n in range(2):
                take_kT(0, n)
            for n in range(2):
                act.wait_ge(s_wf[n], 16)
                act.activation(wf[:, n, :], wf[:, n, :], ACT.Copy, scale=WSCALE).then_inc(s_wfs, 1)
                act.wait_ge(s_wfs, n + 1)
                act.activation(wh[:, n, :], wf[:, n, :], ACT.Copy).then_inc(s_wh, 1)
            act.wait_ge(s_rowsT, 1)
            act.activation(cols[:, :], MISC[:, 0:U + 2 * E], ACT.Copy).then_inc(s_cols, 1)
            take_qr(0, 0)
            for b in range(B):
                for s in range(SLOTS):
                    for pr in range(2):
                        if s < 4 * G:
                            n = PAIRS * b + 2 * s + pr
                            act.wait_ge(st_full, n + 1)
                            if n >= 4:
                                act.wait_ge(av_step, (n - 4) // 2 + 1)
                            act.activation(probs[:, n % 4, :, :], ST[:, n % 2, :, :], ACT.Exp, scale=SCALE).then_inc(exp_done, 1)
                        if pr == 0 and s % 4 == 3 and s // 4 + 1 < G:
                            take_qr(b, s // 4 + 1)
                    if s % 4 == 0 and s >= 4:
                        g = s // 4 - 1
                        act.wait_ge(av_step, 4 * (G * b + g + 1))
                        act.activation(avs[:, g % 2, :], AV[:, :], ACT.Copy).then_inc(av_done, 1)
                act.wait_ge(x2_full, b + 1)
                act.activation(x2h[:, :], MISC[:, :], ACT.Copy).then_inc(x2_done, 1)
                act.activation(x2f[:, :], MISC[:, :], ACT.Copy).then_inc(x2_done, 1)
                act.wait_ge(lg_shift, b + 1)
                act.activation(gexp[:, :, :], lsh[:, :, :], ACT.Exp).then_inc(gexp_done, 1)
                nxt = b + 1 < B
                for u in range(U):
                    v = b * U + u
                    act.wait_ge(up_full, v + 1)
                    if v >= 4:
                        act.wait_ge(hl_done, v - 3)
                    act.activation(hf[:, u % 4, :], UP[u % 2], ACT.Gelu, bias=cols[:, u:u + 1],
                                   scale=1.0 / WSCALE).then_inc(gelu_done, 1)
                    e = u - 8
                    if 0 <= e < E:
                        act.wait_ge(cwb_full, E * b + e + 1)
                        if e == 0 and b >= 1:
                            act.wait_ge(comb_done, E * b)
                        act.activation(cwb[:, e, :], MISC[:, :], ACT.Copy, scale=1.0 / WSCALE).then_inc(cwb_done, 1)
                    if nxt and u == 11:
                        take_xT(b + 1)
                    if nxt and 16 <= u < 21:
                        hi_part(b + 1, u - 16)
                    if nxt and 22 <= u < 24:
                        take_kT(b + 1, u - 22)
                if nxt:
                    take_qr(b + 1, 0)

        @block.vector
        def _(dve):
            chain = [0]

            def link(ins):
                chain[0] += 1
                ins.then_inc(dve_chain, 1)
                dve.wait_ge(dve_chain, chain[0])

            def ln_moments(ln, src):
                for t in range(T):
                    last = dve.bn_stats(stats[:, ln, t, :], src[:, t, :])
                link(last)
                for t in range(T):
                    last = dve.bn_aggr(mv[:, ln, t, :], stats[:, ln, t, :])
                link(last)
                dve.tensor_scalar(ve[:, ln, :], mv[:, ln, :, 1], EPS, None, ALU.add).then_inc(ln_ve, 1)

            def ln_apply(b, ln, src):
                dve.wait_ge(ln_rstd, 2 * b + ln + 1)
                for t in range(T):
                    dve.tensor_scalar(xn[:, ln, t, :], src[:, t, :], mv[:, ln, t, 0:1], rstd[:, ln, t:t + 1],
                                      ALU.subtract, ALU.mult).then_inc(ln_done[ln], 1)

            def add_bias(b, n):
                dve.wait_ge(qk_full, 2 * b + n + 1)
                dve.tensor_tensor(qkf[:, 2 * n:2 * n + 2, :], SM[n][:, :].rearrange("p (t c) -> p t c", t=2),
                                  bqk[:, :].unsqueeze(1).broadcast_to([P, 2, 2 * C]), ALU.add).then_inc(qk_done, 1)

            def lo_part(b, n):
                dve.wait_ge(aug_hi, 5 * b + 2 * n + 1)
                dst, hi, c0 = [(k_aug[:, :, :, 16:24], k_aug[:, :, :, 0:8], C),
                               (q_aug[:, :, :, 8:16], q_aug[:, :, :, 0:8], 0)][n]
                dve.tensor_tensor(dst, qkf[:, :, c0:c0 + C].rearrange("p t (h d) -> p t h d", d=Dh), hi,
                                  ALU.subtract).then_inc(aug_lo, 1)

            def take_qT(b, n):
                dve.wait_ge(qT_full, 2 * b + n + 1)
                dve.tensor_copy(qT0[:, 2 * n:2 * n + 2, :].rearrange("p g n -> p (g n)"), SM16[n]).then_inc(qT_done, 1)

            def row_max(b, m):
                dve.wait_ge(sm_full, SM_N * b + m + 1)
                dve.tensor_reduce(q_aug[:, m % 4, m // 4, 24:25], SM[m % 2][:, :], AX.X, ALU.max,
                                  negate=True).then_inc(sm_max, 1)

            def finish(b):
                dve.wait_ge(fT_full, b + 1)
                if b >= 1:
                    dve.wait_ge(out_dma, 16 * b)
                dve.tensor_tensor(res[:, :, :], x1[:, :, :], MISC[:, :].rearrange("p (t c) -> p t c", t=T),
                                  ALU.add).then_inc(res_done, 1)

            link(dve.memset(q_aug[:, :, :, :].rearrange("p t h r -> p (t h r)").bitcast(U32), 0))
            dve.memset(k_aug[:, :, :, :].rearrange("p t h r -> p (t h r)").bitcast(U32), 0).then_inc(s_aug0, 1)
            dve.wait_ge(x_in, 16)
            ln_moments(0, xt)
            link(dve.memset(v_aug[:, :, :, :], 0.0))
            dve.memset(k_aug[:, :, :, 24:25], 1.0).then_inc(s_aug0, 1)
            dve.memset(v_aug[:, :, :, 8:9], 1.0).then_inc(s_aug0, 1)
            ln_apply(0, 0, xt)
            dve.wait_ge(s_w, 64)
            for n in range(2):
                add_bias(0, n)
            for n in range(2):
                lo_part(0, n)
            for n in range(2):
                take_qT(0, n)
            for m in range(LEAD):
                row_max(0, m)
            dve.wait_ge(s_const, 4)
            dve.tensor_copy(iota8[:, :], iota8i[:, :]).then_inc(s_b2s, 1)
            dve.wait_ge(s_cols, 1)
            dve.tensor_scalar(b2s[:, :], cols[:, U + E:U + 2 * E], WSCALE, None, ALU.mult).then_inc(s_b2s, 1)
            for b in range(B):
                for s in range(SLOTS):
                    for m in range(LEAD + 4 * s, min(LEAD + 4 * s + 4, SM_N)):
                        row_max(b, m)
                    if s == 1 and b >= 1:
                        finish(b - 1)
                    for g in range(G):
                        if s == ot_slot(g):
                            dve.wait_ge(ot_full, G * b + g + 1)
                            ot = MISC[:, :].rearrange("p (t j r) -> p t j r", t=T, r=32)
                            link(dve.reciprocal(rden[:, g % 2, :, :], ot[:, :, :, 8]))
                            cols_g = slice(32 * g, 32 * g + 32)
                            dve.tensor_tensor(att[:, :, cols_g].rearrange("p t (j d) -> p t j d", d=Dh),
                                              ot[:, :, :, 0:8],
                                              rden[:, g % 2, :, :].unsqueeze(3).broadcast_to([P, T, 4, Dh]),
                                              ALU.mult).then_inc(ot_used, 1)
                            dve.wait_ge(ot_used, G * b + g + 1)
                            dve.tensor_tensor(x1[:, :, cols_g], xt[:, :, cols_g], att[:, :, cols_g],
                                              ALU.add).then_inc(x1_done, 1)
                dve.wait_ge(x1_done, G * (b + 1))
                ln_moments(1, x1)
                ln_apply(b, 1, x1)
                dve.wait_ge(x2_done, 2 * (b + 1))
                dve.tensor_tensor(x2l[:, :], x2f[:, :], x2h[:, :], ALU.subtract).then_inc(x2l_done, 1)
                dve.wait_ge(lg_full, b + 1)
                lg = MISC[:, 0:T * E].rearrange("p (t e) -> p t e", e=E)

                def per_tile(a):
                    return a.unsqueeze(2).broadcast_to([P, T, E])

                link(dve.tensor_reduce(nl1[:, :], lg, AX.X, ALU.max))
                dve.tensor_tensor(lsh[:, :, :], lg, per_tile(nl1[:, :]), ALU.subtract).then_inc(lg_shift, 1)
                nxt = b + 1 < B
                for u in range(UNITS):
                    if u < U:
                        v = b * U + u
                        dve.wait_ge(gelu_done, v + 1)
                        if v >= RING:
                            dve.wait_ge(down_done, v - RING + 1)
                        dve.tensor_copy(hh[:, u % RING, :], hf[:, u % 4, :]).then_inc(hh_done, 1)
                    if u == 0:
                        dve.wait_ge(gexp_done, b + 1)
                        link(dve.tensor_reduce(gsum[:, :], gexp[:, :, :], AX.X, ALU.add))
                        link(dve.reciprocal(grec[:, :], gsum[:, :]))
                        link(dve.tensor_tensor(gate[:, :, :], gexp[:, :, :], per_tile(grec[:, :]), ALU.mult))
                    if u == 1:
                        for t in range(T):
                            last = dve.max(top[:, t, :], gate[:, t, :])
                        link(last)
                        for t in range(T):
                            last = dve.max_index(topi[:, t, :], top[:, t, :], gate[:, t, :])
                        link(last)
                    if u == 2:
                        link(dve.tensor_copy(topf[:, :, :], topi[:, :, 0:2]))
                        for r in range(2):
                            last = dve.tensor_tensor(pickd[:, r, :, :], iota8[:, :].unsqueeze(1).broadcast_to([P, T, E]),
                                                     per_tile(topf[:, :, r]), ALU.is_equal)
                        link(last)
                    if u == 3:
                        link(dve.tensor_tensor(pickd[:, 0, :, :], pickd[:, 0, :, :], pickd[:, 1, :, :], ALU.add))
                        link(dve.tensor_tensor(cw[:, :, :], gate[:, :, :], pickd[:, 0, :, :], ALU.mult))
                        link(dve.tensor_copy(cwhl[:, :, 0, :], cw[:, :, :]))
                        dve.tensor_tensor(cwhl[:, :, 1, :], cw[:, :, :], cwhl[:, :, 0, :], ALU.subtract).then_inc(cw_done, 1)
                    if u == 6:
                        dve.wait_ge(cwT_full, b + 1)
                        dve.tensor_copy(cwT[:, :], MISC16[0:2 * E, 0:N]).then_inc(cwT_done, 1)
                    if nxt and u == 5:
                        dve.wait_ge(x_in, 16 * (b + 2))
                        ln_moments(0, xt)
                    if nxt and u == 8:
                        ln_apply(b + 1, 0, xt)
                    if nxt and 13 <= u < 15:
                        add_bias(b + 1, u - 13)
                    if nxt and u in (17, 19):
                        lo_part(b + 1, (u - 17) // 2)
                    if nxt and 23 <= u < 25:
                        take_qT(b + 1, u - 23)
                    if nxt and 26 <= u < 26 + LEAD // 2:
                        row_max(b + 1, 2 * (u - 26))
                        row_max(b + 1, 2 * (u - 26) + 1)
                    w = u - LAG_DN - 1
                    if w >= 0 and w % HC == HC - 1:
                        e = w // HC
                        dve.wait_ge(down_done, b * U + w + 1)
                        dve.wait_ge(cwb_done, E * b + e + 1)
                        if b + e == 0:
                            dve.wait_ge(s_b2s, 2)
                        dst = accT if e == 0 else ytmp
                        if e >= 2:
                            dve.wait_ge(acc_done, (E - 1) * b + e - 1)
                        dve.scalar_tensor_tensor(out=dst[:, :], in0=Y[e % 2], scalar=b2s[:, e:e + 1],
                                                 in1=cwb[:, e, :], op0=ALU.add, op1=ALU.mult).then_inc(comb_done, 1)
                        if e >= 1:
                            dve.wait_ge(comb_done, E * b + e + 1)
                            dve.tensor_tensor(accT[:, :], accT[:, :], ytmp[:, :], ALU.add).then_inc(acc_done, 1)
            finish(B - 1)

        @block.tensor
        def _(pe):
            def turn_x(b):
                for t in range(T):
                    pe.wait_ge(ln_done[0], T * b + t + 1)
                    last = pe.transpose(SM[0][:, P * t:P * t + P], xn[:, 0, t, :], ident[:, :])
                last.then_inc(xT_full, 1)

            def project(b, t):
                pe.wait_ge(xT_done, b + 1)
                mm = pe.matmul(SM[t // 2][:, 256 * (t % 2):256 * (t % 2) + 256], xT[:, P * t:P * t + P],
                               wqk[:, :], start=True, stop=True)
                if t % 2:
                    mm.then_inc(qk_full, 1)

            def turn_k(b, n):
                pe.wait_ge(aug_hi, 5 * b + 2)
                pe.wait_ge(aug_lo, 2 * b + 1)
                for g in (2 * n, 2 * n + 1):
                    for t in range(T):
                        last = pe.transpose(SM16[n][:, N * (g % 2) + P * t:N * (g % 2) + P * t + P],
                                            k_aug[:, t, 4 * g:4 * g + 4, :].rearrange("p h r -> p (h r)"), ident16[:, :])
                last.then_inc(kT_full, 1)

            def turn_q(b, n):
                pe.wait_ge(aug_hi, 5 * b + 4)
                pe.wait_ge(aug_lo, 2 * b + 2)
                pe.wait_ge(kT_done, 2 * b + n + 1)
                for g in (2 * n, 2 * n + 1):
                    for t in range(T):
                        last = pe.transpose(SM16[n][:, N * (g % 2) + P * t:N * (g % 2) + P * t + P],
                                            q_aug[:, t, 4 * g:4 * g + 4, :].rearrange("p h r -> p (h r)"), ident16[:, :])
                last.then_inc(qT_full, 1)

            def score_max(b, m):
                if m == 0:
                    pe.wait_ge(km_in, 64 * (b + 1))
                if m < 2:
                    pe.wait_ge(qT_done, 2 * (b + 1))
                if m >= 2:
                    pe.wait_ge(sm_max, SM_N * b + m - 1)
                h = m // 4
                pe.matmul(SM[m % 2][:, :], qT0[:, h // 4, P * (m % 4):P * (m % 4) + P], kTm[:, h // 4, h % 4, :],
                          start=True, stop=True).then_inc(sm_full, 1)

            def turn_qr(b, g):
                pe.wait_ge(sm_max, SM_N * b + 16 * (g + 1))
                if g >= 2:
                    pe.wait_ge(ot_used, G * b + g - 1)
                if g == 1 and b >= 1:
                    pe.wait_ge(res_done, b)
                if g == 0 and b >= 1:
                    pe.wait_ge(cwb_done, E * b)
                for t in range(T):
                    last = pe.transpose(MISC16[:, P * t:P * t + P],
                                        q_aug[:, t, 4 * g:4 * g + 4, :].rearrange("p h r -> p (h r)"), ident16[:, :])
                last.then_inc(qr_full, 1)

            def score_pair(b, s, pr):
                g, c = s // 4, s % 4
                n = PAIRS * b + 2 * s + pr
                if n >= 2:
                    pe.wait_ge(exp_done, n - 1)
                if s == 0 and b >= 1:
                    pe.wait_ge(comb_done, E * b)
                if c == 0:
                    pe.wait_ge(qr_done, G * b + g + 1)
                for k in (2 * pr, 2 * pr + 1):
                    mm = pe.matmul(ST[:, n % 2, k % 2, :], kTm[:, g, k, P * c:P * c + P], qT1[:, g % 2, :],
                                   start=True, stop=True)
                mm.then_inc(st_full, 1)

            def values(b, s):
                g, c = s // 4, s % 4
                if c == 0 and G * b + g >= 1:
                    pe.wait_ge(av_done, G * b + g)
                for j in range(4):
                    pe.wait_ge(exp_done, PAIRS * b + 2 * s + j // 2 + 1)
                    last = pe.matmul(AV[32 * j:32 * j + 32, :], v_aug[:, c, 4 * g + j, :],
                                     probs[:, (2 * s + j // 2) % 4, j % 2, :], start=(c == 0), stop=(c == T - 1))
                last.then_inc(av_step, 1)

            def turn_out(b, g):
                pe.wait_ge(av_done, G * b + g + 1)
                if g >= 1:
                    pe.wait_ge(ot_used, G * b + g)
                if g + 2 <= G:
                    pe.wait_ge(qr_done, G * b + g + 2)
                for t in range(T):
                    last = pe.transpose(MISC[:, P * t:P * t + P], avs[:, g % 2, P * t:P * t + P], ident[:, :])
                last.then_inc(ot_full, 1)

            def turn_sum(b):
                pe.wait_ge(acc_done, (E - 1) * (b + 1))
                if b + 1 < B:
                    pe.wait_ge(qr_done, G * (b + 1) + 1)
                for t in range(T):
                    last = pe.transpose(MISC[:, P * t:P * t + P], accT[:, P * t:P * t + P], ident[:, :])
                last.then_inc(fT_full, 1)

            pe.wait_ge(s_const, 3)
            turn_x(0)
            pe.wait_ge(s_w, 64)
            for t in range(T):
                project(0, t)
            for n in range(2):
                turn_k(0, n)
            for n in range(2):
                turn_q(0, n)
            pe.wait_ge(s_rows, 48)
            pe.transpose(MISC[:, 0:U + 2 * E], rows[0:U + 2 * E, :], ident[0:U + 2 * E, 0:U + 2 * E]).then_inc(s_rowsT, 1)
            for m in range(LEAD):
                score_max(0, m)
            pe.wait_ge(s_cols, 1)
            turn_qr(0, 0)
            for b in range(B):
                for s in range(SLOTS):
                    sm = [m for m in range(LEAD + 4 * s, min(LEAD + 4 * s + 4, SM_N))]
                    for m in sm[0:1]:
                        score_max(b, m)
                    if s == 1 and b >= 1:
                        turn_sum(b - 1)
                    if s % 4 == 3 and s // 4 + 1 < G:
                        turn_qr(b, s // 4 + 1)
                    for g in range(G):
                        if s == ot_slot(g):
                            turn_out(b, g)
                    if s < 4 * G:
                        score_pair(b, s, 0)
                    for m in sm[1:2]:
                        score_max(b, m)
                    if s < 4 * G:
                        score_pair(b, s, 1)
                    for m in sm[2:3]:
                        score_max(b, m)
                    if 1 <= s <= 4 * G:
                        values(b, s - 1)
                    for m in sm[3:4]:
                        score_max(b, m)
                for t in range(T):
                    pe.wait_ge(ln_done[1], T * b + t + 1)
                    last = pe.transpose(MISC[:, P * t:P * t + P], xn[:, 1, t, :], ident[:, :])
                last.then_inc(x2_full, 1)
                pe.wait_ge(x2_done, 2 * (b + 1))
                for t in range(T):
                    last = pe.matmul(MISC[:, E * t:E * t + E], x2f[:, P * t:P * t + P], cols[:, U:U + E],
                                     start=True, stop=True)
                last.then_inc(lg_full, 1)
                if b == 0:
                    pe.wait_ge(s_wl, 2)
                nxt = b + 1 < B
                for u in range(UNITS):
                    if u < U:
                        v = b * U + u
                        if u >= 2:
                            pe.wait_ge(gelu_done, v - 1)
                        w = slice(P * u, P * u + P)
                        pe.matmul(UP[u % 2], wh[:, 0, w], x2h[:, :], start=True, stop=False)
                        pe.matmul(UP[u % 2], wl[:, 0, w], x2h[:, :], start=False, stop=False)
                        if u == 0:
                            pe.wait_ge(x2l_done, b + 1)
                        pe.matmul(UP[u % 2], wh[:, 0, w], x2l[:, :], start=False, stop=True).then_inc(up_full, 1)
                    if u == 6:
                        pe.wait_ge(cw_done, b + 1)
                        for t in range(T):
                            last = pe.transpose(MISC16[0:2 * E, P * t:P * t + P],
                                                cwhl[:, t, :, :].rearrange("p a e -> p (a e)"), ident16[:, :])
                        last.then_inc(cwT_full, 1)
                    e = u - 8
                    if 0 <= e < E:
                        if e == 0:
                            pe.wait_ge(cwT_done, b + 1)
                        else:
                            pe.wait_ge(cwb_done, E * b + e)
                        pe.matmul(MISC[:, :], pick[:, e, :], cwT[:, :], start=True, stop=True).then_inc(cwb_full, 1)
                    if nxt and u == 10:
                        turn_x(b + 1)
                    if nxt and 12 <= u < 14:
                        project(b + 1, 2 * (u - 12))
                        project(b + 1, 2 * (u - 12) + 1)
                    if nxt and 21 <= u < 23:
                        turn_k(b + 1, u - 21)
                    if nxt and 23 <= u < 25:
                        turn_q(b + 1, u - 23)
                    if nxt and 26 <= u < 26 + LEAD // 2:
                        score_max(b + 1, 2 * (u - 26))
                    w = u - LAG_DN
                    if 0 <= w < U:
                        e, c = w // HC, w % HC
                        v = b * U + w
                        y = Y[e % 2]
                        pe.wait_ge(hh_done, v + 1)
                        if c == 0 and e >= 2:
                            pe.wait_ge(comb_done, E * b + e - 1)
                        ws = slice(P * w, P * w + P)
                        pe.matmul(y, wh[:, 1, ws], hh[:, w % RING, :], start=(c == 0), stop=False)
                        pe.matmul(y, wl[:, 1, ws], hh[:, w % RING, :], start=False, stop=False)
                        pe.wait_ge(hl_done, v + 1)
                        pe.matmul(y, wh[:, 1, ws], hl[:, w % RING, :], start=False, stop=(c == HC - 1)).then_inc(down_done, 1)
                    if nxt and 26 <= u < 26 + LEAD // 2:
                        score_max(b + 1, 2 * (u - 26) + 1)
                if nxt:
                    turn_qr(b + 1, 0)
            turn_sum(B - 1)


_INS = ["L0_attn_x", "L0_attn_Wq", "L0_attn_bq", "L0_attn_Wk", "L0_attn_bk",
        "L0_ffn_w_gate", "L0_ffn_W1", "L0_ffn_b1", "L0_ffn_W2", "L0_ffn_b2"]


def kernel(**inputs):
    import concourse.bacc as bacc
    from concourse.bass_utils import run_bass_kernel_spmd

    nc = bacc.Bacc("TRN2", target_bir_lowering=False, num_devices=1)
    arrays, args = {}, []
    for name in _INS:
        a = np.ascontiguousarray(inputs[name])
        arrays[name] = a
        args.append(nc.dram_tensor(name, a.shape, mybir.dt.from_np(a.dtype), kind="ExternalInput").ap())
    args.append(nc.dram_tensor("out", inputs["L0_attn_x"].shape, F32, kind="ExternalOutput").ap())
    preln_attention_moe(nc, *args)
    r = run_bass_kernel_spmd(nc, [arrays], core_ids=[0])
    return r.results[0]["out"]
```

```python
from contextlib import ExitStack

import numpy as np

import concourse.bass as bass
from concourse import mybir

ALU = mybir.AluOpType
ACT = mybir.ActivationFunctionType
AX = mybir.AxisListType
F32 = mybir.dt.float32
F16 = mybir.dt.float16
U32 = mybir.dt.uint32

P = 128
WSCALE = 64.0
EPS = 1e-5


def preln_attention_moe(nc, x, wq, bq, wk, bk, w_gate, W1, b1, W2, b2, out):
    B, N, C = x.shape
    H, Dh = 16, C // 16
    E, _, F = W1.shape
    T = N // P
    G = H // 4
    HC = F // P
    RING = 8
    U = E * HC
    SCALE = float(C) ** -0.5
    assert C == P and Dh == 8 and N == 512

    with ExitStack() as ctx:
        def sb(name, shape, dt):
            return ctx.enter_context(nc.sbuf_tensor(name, shape, dt))

        def psum(name, shape, dt):
            return ctx.enter_context(nc.psum_tensor(name, shape, dt))

        def sem(name):
            return ctx.enter_context(nc.semaphore(name))

        ident = sb("ident", [P, P], F32)
        ident16 = sb("ident16", [P, P], F16)
        iota8 = sb("iota8", [P, E], F32)
        iota8i = sb("iota8i", [P, E], mybir.dt.int32)
        neg_half = sb("neg_half", [P, T], F32)
        pick = sb("pick", [2 * E, E, P], F16)
        wqk = sb("wqk", [P, 2 * C], F32)
        bqk = sb("bqk", [P, 2 * C], F32)
        rows = sb("rows", [P, P], F32)
        cols = sb("cols", [P, U + 2 * E], F32)
        b2s = sb("b2s", [P, E], F32)
        wf = sb("wf", [P, 2, U * P], F32)
        wh = sb("wh", [P, 2, U * P], F16)
        wl = sb("wl", [P, 2, U * P], F16)

        xt = sb("xt", [P, 2, T, C], F32)
        stats = sb("stats", [P, 2, T, 6], F32)
        mv = sb("mv", [P, 2, T, 2], F32)
        ve = sb("ve", [P, 2, T], F32)
        rstd = sb("rstd", [P, 2, T], F32)
        xn = sb("xn", [P, 2, T, C], F32)
        xT = sb("xT", [P, N], F32)
        qkf = sb("qkf", [P, T, 2 * C], F32)
        q_aug = sb("q_aug", [P, T, H, 32], F16)
        k_aug = sb("k_aug", [P, T, H, 32], F16)
        v_aug = sb("v_aug", [P, T, H, 32], F32)
        qT0 = sb("qT0", [P, G, N], F16)
        qT1 = sb("qT1", [P, 2, N], F16)
        kT = sb("kT", [P, G, N], F16)
        kTm = sb("kTm", [P, G, 4, N], F16)
        probs = sb("probs", [P, 4, 2, N], F32)
        avs = sb("avs", [P, 2, N], F32)
        rden = sb("rden", [P, 2, T, 4], F32)
        att = sb("att", [P, T, C], F32)
        x1 = sb("x1", [P, T, C], F32)
        x2f = sb("x2f", [P, N], F32)
        x2h = sb("x2h", [P, N], F16)
        x2l = sb("x2l", [P, N], F16)
        nl1 = sb("nl1", [P, T], F32)
        lsh = sb("lsh", [P, T, E], F32)
        gexp = sb("gexp", [P, T, E], F32)
        gsum = sb("gsum", [P, T], F32)
        grec = sb("grec", [P, T], F32)
        gate = sb("gate", [P, T, E], F32)
        top = sb("top", [P, T, 8], F32)
        topi = sb("topi", [P, T, 8], U32)
        topf = sb("topf", [P, T, 2], F32)
        pickd = sb("pickd", [P, 2, T, E], F32)
        cw = sb("cw", [P, T, E], F32)
        cwhl = sb("cwhl", [P, T, 2, E], F16)
        cwT = sb("cwT", [2 * E, N], F16)
        hf = sb("hf", [P, 4, N], F32)
        hh = sb("hh", [P, RING, N], F16)
        hl = sb("hl", [P, RING, N], F16)
        x1_prev = sb("x1_prev", [P, T, C], F32)
        ytmp = sb("ytmp", [P, 2, N], F32)
        accT = sb("accT", [P, N], F32)
        res = sb("res", [P, T, C], F32)

        cwb = wf[:, 0, :].rearrange("p (e n) -> p e n", e=E)

        SM = [psum(f"SM{i}", [P, N], F32) for i in range(2)]
        ST = psum("ST", [P, 2, 2, N], F32)
        AV = psum("AV", [P, N], F32)
        MISC = psum("MISC", [P, N], F32)
        MISC16 = MISC[:, :].bitcast(F16)
        SM16 = [s[:, :].bitcast(F16) for s in SM]
        UP = [ST[:, 0, i, :] for i in range(2)]
        Y = [ST[:, 1, i, :] for i in range(2)]

        s_const = sem("s_const")
        s_w = sem("s_w")
        s_rows = sem("s_rows")
        s_wf = [sem("s_w1"), sem("s_w2")]
        s_rowsT = sem("s_rowsT")
        s_cols = sem("s_cols")
        s_b2s = sem("s_b2s")
        s_wfs = sem("s_wfs")
        s_wh = sem("s_wh")
        s_wl = sem("s_wl")
        x_in = sem("x_in")
        ln_ve = [sem("ln1_ve"), sem("ln2_ve")]
        ln_rstd = [sem("ln1_rstd"), sem("ln2_rstd")]
        ln_done = [sem("ln1_done"), sem("ln2_done")]
        xT_full = sem("xT_full")
        xT_done = sem("xT_done")
        qk_full = sem("qk_full")
        qk_done = sem("qk_done")
        aug_hi = sem("aug_hi")
        aug_lo = sem("aug_lo")
        s_aug0 = sem("s_aug0")
        s_kTm = sem("s_kTm")
        kT_full = sem("kT_full")
        kT_done = sem("kT_done")
        qT_full = sem("qT_full")
        qT_done = sem("qT_done")
        km_in = [sem("km01_in"), sem("km23_in")]
        sm_full = sem("sm_full")
        sm_max = sem("sm_max")
        qr_full = sem("qr_full")
        qr_done = sem("qr_done")
        st_full = sem("st_full")
        exp_done = sem("exp_done")
        av_step = sem("av_step")
        av_done = sem("av_done")
        ot_full = sem("ot_full")
        ot_used = sem("ot_used")
        x1_done = sem("x1_done")
        x2_full = sem("x2_full")
        x2_done = sem("x2_done")
        x2l_done = sem("x2l_done")
        lg_full = sem("lg_full")
        lg_shift = sem("lg_shift")
        gexp_done = sem("gexp_done")
        cw_done = sem("cw_done")
        cwT_full = sem("cwT_full")
        cwT_done = sem("cwT_done")
        cwb_full = sem("cwb_full")
        cwb_done = sem("cwb_done")
        up_full = sem("up_full")
        gelu_done = sem("gelu_done")
        hh_done = sem("hh_done")
        hl_done = sem("hl_done")
        down_done = sem("down_done")
        comb_done = sem("comb_done")
        acc_done = sem("acc_done")
        fT_full = sem("fT_full")
        res_done = sem("res_done")
        x1p_done = sem("x1p_done")
        out_dma = sem("out_dma")
        dve_chain = sem("dve_chain")
        pool_chain = sem("pool_chain")

        SLOTS = 4 * G + 2
        SM_N = 4 * H
        PAIRS = G * 4 * 2
        LAG_DN = 4
        DEFER = 2 * HC
        QR = [-1, 3, 7, 11]

        def lead(b):
            return 16 if b == 0 else 32

        def sm_of_slot(b, s):
            if b == 0:
                starts = list(range(lead(0), SM_N, 4))
            else:
                starts = list(range(32, SM_N, 3)) + [SM_N]
            starts += [SM_N] * (SLOTS + 1)
            return list(range(starts[s], min(starts[s + 1], SM_N)))

        W_CHUNKS = 16

        def w_chunk(i):
            half = W_CHUNKS // 2
            w = U * P // half
            return i // half, slice(w * (i % half), w * (i % half) + w)

        SM_FROM = 4

        def sm_of_unit(u):
            starts = [0]
            while len(starts) <= U:
                u_ = len(starts) - 1
                starts.append(min(starts[-1] + (0 if u_ < SM_FROM else 2 if u_ % 4 == 3 and 11 <= u_ < 24 else 1), 32))
            return list(range(starts[u], starts[u + 1])) if u < U else []

        def steps(b):
            return max(U, units_down(b) + LAG_DN)

        def units_down(b):
            return U if b == B - 1 else U - DEFER

        def ot_slot(g):
            return 4 * g + 6 if g < G - 1 else SLOTS - 1

        block = ctx.enter_context(nc.Block())

        @block.sync
        def _(sp):
            sp.dma_start(xt[:, 0, :, :], x[0].rearrange("(t p) c -> p t c", p=P)).then_inc(x_in, 16)
            sp.dma_start(wqk[:, 0:C], wq).then_inc(s_w, 16)
            sp.dma_start(wqk[:, C:2 * C], wk).then_inc(s_w, 16)
            sp.dma_start(bqk[:, 0:C], bq.partition_broadcast(P)).then_inc(s_w, 16)
            sp.dma_start(bqk[:, C:2 * C], bk.partition_broadcast(P)).then_inc(s_w, 16)
            sp.dma_start(wf[:, 0, :].rearrange("p (e h) -> p e h", e=E), W1.rearrange("e d h -> d e h")).then_inc(s_wf[0], 16)
            sp.dma_start(rows[0:U, :], b1.rearrange("e (c h) -> (e c) h", h=P)).then_inc(s_rows, 16)
            sp.dma_start(rows[U:U + E, :], w_gate).then_inc(s_rows, 16)
            sp.dma_start(rows[U + E:U + 2 * E, :], b2).then_inc(s_rows, 16)
            sp.dma_start(wf[:, 1, :].rearrange("p (e c d) -> p e c d", e=E, c=HC),
                         W2.rearrange("e (c p) d -> p e c d", p=P)).then_inc(s_wf[1], 16)
            for b in range(B):
                if b == 0:
                    sp.wait_ge(s_kTm, 1)
                for n in range(2):
                    sp.wait_ge(kT_done, 2 * b + n + 1)
                    gs = slice(2 * n, 2 * n + 2)
                    for j in range(4):
                        sp.dma_start(kTm[32 * j:32 * j + 32, gs, j, :], kT[32 * j:32 * j + 32, gs, :]).then_inc(km_in[n], 16)
                if b >= 2:
                    sp.wait_ge(res_done, b - 1)
                    sp.dma_start(out[b - 2].rearrange("(t p) c -> p t c", p=P), res[:, :, :]).then_inc(out_dma, 16)
                if b + 1 < B:
                    if b >= 1:
                        sp.wait_ge(x1_done, G * b)
                    sp.dma_start(xt[:, (b + 1) % 2, :, :], x[b + 1].rearrange("(t p) c -> p t c", p=P)).then_inc(x_in, 16)
            sp.wait_ge(res_done, B - 1)
            sp.dma_start(out[B - 2].rearrange("(t p) c -> p t c", p=P), res[:, :, :]).then_inc(out_dma, 16)
            sp.wait_ge(res_done, B)
            sp.dma_start(out[B - 1].rearrange("(t p) c -> p t c", p=P), res[:, :, :]).then_inc(out_dma, 16)
            sp.wait_ge(out_dma, 16 * B)

        @block.gpsimd
        def _(pool):
            chain = [0]

            def link(ins):
                chain[0] += 1
                ins.then_inc(pool_chain, 1)
                pool.wait_ge(pool_chain, chain[0])

            def inv_sqrt(b, ln):
                pool.wait_ge(ln_ve[ln], b + 1)
                pool.tensor_tensor(rstd[:, ln, :], ve[:, ln, :], neg_half[:, :], ALU.pow).then_inc(ln_rstd[ln], 1)

            link(pool.memset(ident[:, :], 0.0))
            pool.memset(neg_half[:, :], -0.5).then_inc(s_const, 1)
            pool.affine_select(out=ident[:, :], in_=ident[:, :], compare_op=ALU.not_equal, fill=1.0,
                               base=0, pattern=[[-1, P]], channel_multiplier=1).then_inc(s_const, 1)
            pool.wait_ge(s_const, 2)
            pool.tensor_copy(ident16[:, :], ident[:, :]).then_inc(s_const, 1)
            inv_sqrt(0, 0)
            pool.memset(kTm[:, :, :, :], 0.0).then_inc(s_kTm, 1)
            pool.iota(iota8i[:, :], pattern=[[1, E]], base=0, channel_multiplier=0).then_inc(s_const, 1)
            link(pool.memset(pick[:, :, :], 0.0))
            for half in range(2):
                link(pool.affine_select(out=pick[:, :, :], in_=pick[:, :, :], compare_op=ALU.not_equal, fill=1.0,
                                        base=-half * E, pattern=[[-1, E], [0, P]], channel_multiplier=1))
            for n in range(2):
                pool.wait_ge(s_wf[n], 16)
                pool.tensor_scalar(wf[:, n, :], wf[:, n, :], WSCALE, None, ALU.mult).then_inc(s_wfs, 1)
            for i in range(W_CHUNKS):
                n, cs = w_chunk(i)
                pool.wait_ge(s_wh, i + 1)
                pool.tensor_tensor(wl[:, n, cs], wf[:, n, cs], wh[:, n, cs], ALU.subtract).then_inc(s_wl, 1)
                if i == 10 and B > 1:
                    inv_sqrt(1, 0)
            def add_expert(b, e):
                pool.wait_ge(comb_done, E * b + e + 1)
                if e >= 2:
                    pool.wait_ge(acc_done, (E - 1) * b + e - 1)
                pool.tensor_tensor(accT[:, :], accT[:, :], ytmp[:, e % 2, :], ALU.add).then_inc(acc_done, 1)

            for b in range(B):
                if 1 <= b < B - 1:
                    inv_sqrt(b + 1, 0)
                inv_sqrt(b, 1)
                if b >= 1:
                    add_expert(b - 1, E - 2)
                for u in range(U):
                    v = b * U + u
                    pool.wait_ge(gelu_done, v + 1)
                    pool.wait_ge(hh_done, v + 1)
                    if v >= RING:
                        pool.wait_ge(down_done, v - RING + 1)
                    pool.tensor_tensor(hl[:, u % RING, :], hf[:, u % 4, :], hh[:, u % RING, :],
                                       ALU.subtract).then_inc(hl_done, 1)
                    if b >= 1 and u == 1:
                        add_expert(b - 1, E - 1)
                    w = u - LAG_DN - 2
                    if b < B - 1 and w >= 0 and w % HC == HC - 1 and w >= HC:
                        add_expert(b, w // HC)
                for e in range((U - LAG_DN - 2) // HC, units_down(b) // HC if b < B - 1 else 0):
                    add_expert(b, e)
                if b + 1 < B:
                    pool.wait_ge(x1_done, G * (b + 1))
                    pool.tensor_copy(x1_prev[:, :, :], x1[:, :, :]).then_inc(x1p_done, 1)

        @block.scalar
        def _(act):
            qv = qkf[:, :, 0:C].rearrange("p t (h d) -> p t h d", d=Dh)
            kv = qkf[:, :, C:2 * C].rearrange("p t (h d) -> p t h d", d=Dh)

            def hi_part(b, n):
                act.wait_ge(qk_done, 2 * (b + 1))
                if b == 0:
                    act.wait_ge(s_aug0, 3)
                dst, src = [(k_aug[:, :, :, 0:8], kv), (k_aug[:, :, :, 8:16], kv), (q_aug[:, :, :, 0:8], qv),
                            (q_aug[:, :, :, 16:24], qv), (v_aug[:, :, :, 0:8], kv)][n]
                act.activation(dst, src, ACT.Copy).then_inc(aug_hi, 1)

            def take_kT(b, n):
                act.wait_ge(kT_full, 2 * b + n + 1)
                act.activation(kT[:, 2 * n:2 * n + 2, :].rearrange("p g n -> p (g n)"), SM16[n],
                               ACT.Copy).then_inc(kT_done, 1)

            def take_qr(b, g):
                act.wait_ge(qr_full, G * b + g + 1)
                act.activation(qT1[:, g % 2, :], MISC16[:, 0:N], ACT.Copy).then_inc(qr_done, 1)

            for n in range(4):
                hi_part(0, n)
            for n in range(2):
                take_kT(0, n)
            hi_part(0, 4)
            act.wait_ge(s_rowsT, 1)
            act.activation(cols[:, :], MISC[:, 0:U + 2 * E], ACT.Copy).then_inc(s_cols, 1)
            take_qr(0, 0)
            for b in range(B):
                for s in range(SLOTS):
                    for pr in range(2):
                        if s < 4 * G:
                            n = PAIRS * b + 2 * s + pr
                            act.wait_ge(st_full, n + 1)
                            if n >= 4:
                                act.wait_ge(av_step, (n - 4) // 2 + 1)
                            act.activation(probs[:, n % 4, :, :], ST[:, n % 2, :, :], ACT.Exp, scale=SCALE).then_inc(exp_done, 1)
                        if pr == 0 and s % 4 == 3 and s // 4 + 1 < G:
                            take_qr(b, s // 4 + 1)
                    if b == 0 and s < W_CHUNKS:
                        n, cs = w_chunk(s)
                        act.wait_ge(s_wfs, n + 1)
                        act.activation(wh[:, n, cs], wf[:, n, cs], ACT.Copy).then_inc(s_wh, 1)
                    if s == 4 * G and b + 1 < B:
                        for n in range(2):
                            hi_part(b + 1, n)
                    if s % 4 == 0 and s >= 4:
                        g = s // 4 - 1
                        act.wait_ge(av_step, 4 * (G * b + g + 1))
                        act.activation(avs[:, g % 2, :], AV[:, :], ACT.Copy).then_inc(av_done, 1)
                nxt = b + 1 < B
                if nxt:
                    for n in range(2, 5):
                        hi_part(b + 1, n)
                    for n in range(2):
                        take_kT(b + 1, n)
                act.wait_ge(x2_full, b + 1)
                act.activation(x2f[:, :], MISC[:, :], ACT.Copy).then_inc(x2_done, 1)
                act.activation(x2h[:, :], MISC[:, :], ACT.Copy).then_inc(x2_done, 1)
                act.wait_ge(lg_shift, b + 1)
                act.activation(gexp[:, :, :], lsh[:, :, :], ACT.Exp).then_inc(gexp_done, 1)
                for u in range(U):
                    v = b * U + u
                    act.wait_ge(up_full, v + 1)
                    if v >= 4:
                        act.wait_ge(hl_done, v - 3)
                    act.activation(hf[:, u % 4, :], UP[u % 2], ACT.Gelu, bias=cols[:, u:u + 1],
                                   scale=1.0 / WSCALE).then_inc(gelu_done, 1)
                    if nxt and u == U - 4:
                        take_qr(b + 1, 0)
                    e = u - 8
                    if 0 <= e < E:
                        act.wait_ge(cwb_full, E * b + e + 1)
                        if e == 0 and b >= 1:
                            act.wait_ge(comb_done, E * b)
                        act.activation(cwb[:, e, :], MISC[:, :], ACT.Copy, scale=1.0 / WSCALE).then_inc(cwb_done, 1)

        @block.vector
        def _(dve):
            chain = [0]

            def link(ins):
                chain[0] += 1
                ins.then_inc(dve_chain, 1)
                dve.wait_ge(dve_chain, chain[0])

            def ln_moments(ln, src):
                for t in range(T):
                    last = dve.bn_stats(stats[:, ln, t, :], src[:, t, :])
                link(last)
                for t in range(T):
                    last = dve.bn_aggr(mv[:, ln, t, :], stats[:, ln, t, :])
                link(last)
                dve.tensor_scalar(ve[:, ln, :], mv[:, ln, :, 1], EPS, None, ALU.add).then_inc(ln_ve[ln], 1)

            def ln_apply(b, ln, src):
                dve.wait_ge(ln_rstd[ln], b + 1)
                for t in range(T):
                    dve.tensor_scalar(xn[:, ln, t, :], src[:, t, :], mv[:, ln, t, 0:1], rstd[:, ln, t:t + 1],
                                      ALU.subtract, ALU.mult).then_inc(ln_done[ln], 1)

            def add_bias(b, n):
                dve.wait_ge(qk_full, 2 * b + n + 1)
                dve.tensor_tensor(qkf[:, 2 * n:2 * n + 2, :], SM[n][:, :].rearrange("p (t c) -> p t c", t=2),
                                  bqk[:, :].unsqueeze(1).broadcast_to([P, 2, 2 * C]), ALU.add).then_inc(qk_done, 1)

            def lo_part(b, n):
                dve.wait_ge(aug_hi, 5 * b + 2 * n + 1)
                dst, hi, c0 = [(k_aug[:, :, :, 16:24], k_aug[:, :, :, 0:8], C),
                               (q_aug[:, :, :, 8:16], q_aug[:, :, :, 0:8], 0)][n]
                dve.tensor_tensor(dst, qkf[:, :, c0:c0 + C].rearrange("p t (h d) -> p t h d", d=Dh), hi,
                                  ALU.subtract).then_inc(aug_lo, 1)

            def take_qT(b, n):
                dve.wait_ge(qT_full, 2 * b + n + 1)
                dve.tensor_copy(qT0[:, 2 * n:2 * n + 2, :].rearrange("p g n -> p (g n)"), SM16[n]).then_inc(qT_done, 1)

            def row_max(b, m):
                dve.wait_ge(sm_full, SM_N * b + m + 1)
                dve.tensor_reduce(q_aug[:, m % 4, m // 4, 24:25], SM[m % 2][:, :], AX.X, ALU.max,
                                  negate=True).then_inc(sm_max, 1)

            def first_row_max(m):
                dve.wait_ge(sm_full, m + 2)
                t = m % 4
                dve.tensor_reduce(q_aug[:, t:t + 2, m // 4, 24], ST[:, m // 2 % 2, :, :], AX.X, ALU.max,
                                  negate=True).then_inc(sm_max, 2)

            def take_xT(b):
                dve.wait_ge(xT_full, b + 1)
                dve.tensor_copy(xT[:, :], SM[0][:, :]).then_inc(xT_done, 1)

            def combine(b, e):
                dve.wait_ge(down_done, b * U + HC * (e + 1))
                dve.wait_ge(cwb_done, E * b + e + 1)
                if b + e == 0:
                    dve.wait_ge(s_b2s, 2)
                if e == 0 and b >= 1:
                    dve.wait_ge(fT_full, b)
                if e >= 3:
                    dve.wait_ge(acc_done, (E - 1) * b + e - 2)
                dst = accT[:, :] if e == 0 else ytmp[:, e % 2, :]
                dve.scalar_tensor_tensor(out=dst, in0=Y[e % 2], scalar=b2s[:, e:e + 1],
                                         in1=cwb[:, e, :], op0=ALU.add, op1=ALU.mult).then_inc(comb_done, 1)
                if b == B - 1 and e >= 1:
                    dve.wait_ge(comb_done, E * b + e + 1)
                    dve.tensor_tensor(accT[:, :], accT[:, :], ytmp[:, e % 2, :], ALU.add).then_inc(acc_done, 1)

            def finish(b):
                dve.wait_ge(fT_full, b + 1)
                if b >= 1:
                    dve.wait_ge(out_dma, 16 * b)
                if b + 1 < B:
                    dve.wait_ge(x1p_done, b + 1)
                src = x1_prev if b + 1 < B else x1
                dve.tensor_tensor(res[:, :, :], src[:, :, :], MISC[:, :].rearrange("p (t c) -> p t c", t=T),
                                  ALU.add).then_inc(res_done, 1)

            link(dve.memset(q_aug[:, :, :, :].rearrange("p t h r -> p (t h r)").bitcast(U32), 0))
            dve.memset(k_aug[:, :, :, :].rearrange("p t h r -> p (t h r)").bitcast(U32), 0).then_inc(s_aug0, 1)
            dve.wait_ge(x_in, 16)
            ln_moments(0, xt[:, 0, :, :])
            dve.memset(k_aug[:, :, :, 24:25], 1.0).then_inc(s_aug0, 1)
            ln_apply(0, 0, xt[:, 0, :, :])
            take_xT(0)
            link(dve.memset(v_aug[:, :, :, :], 0.0))
            dve.memset(v_aug[:, :, :, 8:9], 1.0).then_inc(s_aug0, 1)
            dve.wait_ge(s_w, 64)
            for n in range(2):
                add_bias(0, n)
            for n in range(2):
                lo_part(0, n)
            for n in range(2):
                take_qT(0, n)
            for m in range(0, lead(0), 2):
                first_row_max(m)
            dve.wait_ge(s_const, 4)
            dve.tensor_copy(iota8[:, :], iota8i[:, :]).then_inc(s_b2s, 1)
            dve.wait_ge(s_cols, 1)
            dve.tensor_scalar(b2s[:, :], cols[:, U + E:U + 2 * E], WSCALE, None, ALU.mult).then_inc(s_b2s, 1)
            for b in range(B):
                nxt = b + 1 < B
                for s in range(SLOTS):
                    for m in sm_of_slot(b, s):
                        row_max(b, m)
                    if nxt and s == 11:
                        dve.wait_ge(x_in, 16 * (b + 2))
                        ln_moments(0, xt[:, (b + 1) % 2, :, :])
                    if nxt and s == 12:
                        ln_apply(b + 1, 0, xt[:, (b + 1) % 2, :, :])
                    if nxt and s == 13:
                        take_xT(b + 1)
                    if nxt and s in (15, 16):
                        add_bias(b + 1, s - 15)
                    if nxt and s == 16:
                        lo_part(b + 1, 0)
                    for g in range(G):
                        if s == ot_slot(g):
                            dve.wait_ge(ot_full, G * b + g + 1)
                            ot = MISC[:, :].rearrange("p (t j r) -> p t j r", t=T, r=32)
                            link(dve.reciprocal(rden[:, g % 2, :, :], ot[:, :, :, 8]))
                            cols_g = slice(32 * g, 32 * g + 32)
                            dve.tensor_tensor(att[:, :, cols_g].rearrange("p t (j d) -> p t j d", d=Dh),
                                              ot[:, :, :, 0:8],
                                              rden[:, g % 2, :, :].unsqueeze(3).broadcast_to([P, T, 4, Dh]),
                                              ALU.mult).then_inc(ot_used, 1)
                            dve.wait_ge(ot_used, G * b + g + 1)
                            if b >= 1 and g == 0:
                                dve.wait_ge(x1p_done, b)
                            dve.tensor_tensor(x1[:, :, cols_g], xt[:, b % 2, :, cols_g], att[:, :, cols_g],
                                              ALU.add).then_inc(x1_done, 1)
                dve.wait_ge(x1_done, G * (b + 1))
                ln_moments(1, x1)
                if nxt:
                    lo_part(b + 1, 1)
                ln_apply(b, 1, x1)
                if b >= 1:
                    combine(b - 1, E - 2)
                if nxt:
                    take_qT(b + 1, 0)
                dve.wait_ge(x2_done, 2 * (b + 1))
                dve.tensor_tensor(x2l[:, :], x2f[:, :], x2h[:, :], ALU.subtract).then_inc(x2l_done, 1)
                dve.wait_ge(lg_full, b + 1)
                lg = AV[:, 0:T * E].rearrange("p (t e) -> p t e", e=E)

                def per_tile(a):
                    return a.unsqueeze(2).broadcast_to([P, T, E])

                link(dve.tensor_reduce(nl1[:, :], lg, AX.X, ALU.max))
                dve.tensor_tensor(lsh[:, :, :], lg, per_tile(nl1[:, :]), ALU.subtract).then_inc(lg_shift, 1)
                if nxt:
                    take_qT(b + 1, 1)
                for u in range(steps(b) + 1):
                    if u < U:
                        v = b * U + u
                        dve.wait_ge(gelu_done, v + 1)
                        if v >= RING:
                            dve.wait_ge(down_done, v - RING + 1)
                        dve.tensor_copy(hh[:, u % RING, :], hf[:, u % 4, :]).then_inc(hh_done, 1)
                    if u == 0:
                        dve.wait_ge(gexp_done, b + 1)
                        link(dve.tensor_reduce(gsum[:, :], gexp[:, :, :], AX.X, ALU.add))
                        link(dve.reciprocal(grec[:, :], gsum[:, :]))
                        link(dve.tensor_tensor(gate[:, :, :], gexp[:, :, :], per_tile(grec[:, :]), ALU.mult))
                    if u == 1:
                        for t in range(T):
                            last = dve.max(top[:, t, :], gate[:, t, :])
                        link(last)
                        for t in range(T):
                            last = dve.max_index(topi[:, t, :], top[:, t, :], gate[:, t, :])
                        link(last)
                    if u == 2:
                        link(dve.tensor_copy(topf[:, :, :], topi[:, :, 0:2]))
                        for r in range(2):
                            last = dve.tensor_tensor(pickd[:, r, :, :], iota8[:, :].unsqueeze(1).broadcast_to([P, T, E]),
                                                     per_tile(topf[:, :, r]), ALU.is_equal)
                        link(last)
                    if u == 3:
                        link(dve.tensor_tensor(pickd[:, 0, :, :], pickd[:, 0, :, :], pickd[:, 1, :, :], ALU.add))
                        link(dve.tensor_tensor(cw[:, :, :], gate[:, :, :], pickd[:, 0, :, :], ALU.mult))
                        link(dve.tensor_copy(cwhl[:, :, 0, :], cw[:, :, :]))
                        dve.tensor_tensor(cwhl[:, :, 1, :], cw[:, :, :], cwhl[:, :, 0, :], ALU.subtract).then_inc(cw_done, 1)
                    if u == 7:
                        dve.wait_ge(cwT_full, b + 1)
                        dve.tensor_copy(cwT[:, :], MISC16[0:2 * E, 0:N]).then_inc(cwT_done, 1)
                    if b >= 1 and u == 1:
                        combine(b - 1, E - 1)
                    if b >= 1 and u == 5:
                        finish(b - 1)
                    if nxt:
                        for m in sm_of_unit(u):
                            row_max(b + 1, m)
                    w = u - LAG_DN - 1
                    if 0 <= w < units_down(b) and w % HC == HC - 1:
                        combine(b, w // HC)
            finish(B - 1)

        @block.tensor
        def _(pe):
            def turn_x(b):
                for t in range(T):
                    pe.wait_ge(ln_done[0], T * b + t + 1)
                    last = pe.transpose(SM[0][:, P * t:P * t + P], xn[:, 0, t, :], ident[:, :])
                last.then_inc(xT_full, 1)

            def project(b, t):
                pe.wait_ge(xT_done, b + 1)
                mm = pe.matmul(SM[t // 2][:, 256 * (t % 2):256 * (t % 2) + 256], xT[:, P * t:P * t + P],
                               wqk[:, :], start=True, stop=True)
                if t % 2:
                    mm.then_inc(qk_full, 1)

            def turn_k(b, n):
                pe.wait_ge(aug_hi, 5 * b + 2)
                pe.wait_ge(aug_lo, 2 * b + 1)
                for g in (2 * n, 2 * n + 1):
                    for t in range(T):
                        last = pe.transpose(SM16[n][:, N * (g % 2) + P * t:N * (g % 2) + P * t + P],
                                            k_aug[:, t, 4 * g:4 * g + 4, :].rearrange("p h r -> p (h r)"), ident16[:, :])
                last.then_inc(kT_full, 1)

            def turn_q(b, n):
                pe.wait_ge(aug_hi, 5 * b + 4)
                pe.wait_ge(aug_lo, 2 * b + 2)
                pe.wait_ge(kT_done, 2 * b + n + 1)
                for g in (2 * n, 2 * n + 1):
                    for t in range(T):
                        last = pe.transpose(SM16[n][:, N * (g % 2) + P * t:N * (g % 2) + P * t + P],
                                            q_aug[:, t, 4 * g:4 * g + 4, :].rearrange("p h r -> p (h r)"), ident16[:, :])
                last.then_inc(qT_full, 1)

            def score_max(b, m):
                if m % 32 == 0 or (b == 0 and m == lead(0)):
                    pe.wait_ge(km_in[m // 32], 64 * (b + 1))
                if m == 0 or (b == 0 and m == lead(0)):
                    pe.wait_ge(qT_done, 2 * (b + 1))
                if m >= 2:
                    pe.wait_ge(sm_max, SM_N * b + m - 1)
                h = m // 4
                pe.matmul(SM[m % 2][:, :], qT0[:, h // 4, P * (m % 4):P * (m % 4) + P], kTm[:, h // 4, h % 4, :],
                          start=True, stop=True).then_inc(sm_full, 1)

            def first_score_max(m):
                if m == 0:
                    pe.wait_ge(kT_done, 1)
                    pe.wait_ge(qT_done, 1)
                if m >= 4:
                    pe.wait_ge(sm_max, m - 2)
                rows_h = slice(32 * (m // 4), 32 * (m // 4) + 32)
                for t in (m % 4, m % 4 + 1):
                    pe.matmul(ST[:, m // 2 % 2, t % 2, :], qT0[rows_h, 0, P * t:P * t + P], kT[rows_h, 0, :],
                              start=True, stop=True).then_inc(sm_full, 1)

            def turn_qr(b, g):
                pe.wait_ge(sm_max, SM_N * b + 16 * (g + 1))
                if g >= 2:
                    pe.wait_ge(ot_used, G * b + g - 1)
                if g == 0 and b >= 1:
                    pe.wait_ge(cwb_done, E * b)
                for t in range(T):
                    last = pe.transpose(MISC16[:, P * t:P * t + P],
                                        q_aug[:, t, 4 * g:4 * g + 4, :].rearrange("p h r -> p (h r)"), ident16[:, :])
                last.then_inc(qr_full, 1)

            def score_pair(b, s, pr):
                g, c = s // 4, s % 4
                n = PAIRS * b + 2 * s + pr
                if n >= 2:
                    pe.wait_ge(exp_done, n - 1)
                if s == 0 and b >= 1:
                    pe.wait_ge(gelu_done, U * b) if pr == 0 else pe.wait_ge(comb_done, E * b - DEFER // HC)
                if c == 0:
                    pe.wait_ge(qr_done, G * b + g + 1)
                for k in (2 * pr, 2 * pr + 1):
                    mm = pe.matmul(ST[:, n % 2, k % 2, :], kTm[:, g, k, P * c:P * c + P], qT1[:, g % 2, :],
                                   start=True, stop=True)
                mm.then_inc(st_full, 1)

            def values(b, s):
                g, c = s // 4, s % 4
                if c == 0 and G * b + g >= 1:
                    pe.wait_ge(av_done, G * b + g)
                for j in range(4):
                    pe.wait_ge(exp_done, PAIRS * b + 2 * s + j // 2 + 1)
                    last = pe.matmul(AV[32 * j:32 * j + 32, :], v_aug[:, c, 4 * g + j, :],
                                     probs[:, (2 * s + j // 2) % 4, j % 2, :], start=(c == 0), stop=(c == T - 1))
                last.then_inc(av_step, 1)

            def turn_out(b, g):
                pe.wait_ge(av_done, G * b + g + 1)
                if g >= 1:
                    pe.wait_ge(ot_used, G * b + g)
                if g + 2 <= G:
                    pe.wait_ge(qr_done, G * b + g + 2)
                for t in range(T):
                    last = pe.transpose(MISC[:, P * t:P * t + P], avs[:, g % 2, P * t:P * t + P], ident[:, :])
                last.then_inc(ot_full, 1)

            def turn_sum(b):
                pe.wait_ge(acc_done, (E - 1) * (b + 1))
                for t in range(T):
                    last = pe.transpose(MISC[:, P * t:P * t + P], accT[:, P * t:P * t + P], ident[:, :])
                last.then_inc(fT_full, 1)

            pe.wait_ge(s_const, 3)
            turn_x(0)
            pe.wait_ge(s_w, 64)
            for t in range(T):
                project(0, t)
            for n in range(2):
                turn_k(0, n)
            for n in range(2):
                turn_q(0, n)
            pe.wait_ge(s_rows, 48)
            pe.transpose(MISC[:, 0:U + 2 * E], rows[0:U + 2 * E, :], ident[0:U + 2 * E, 0:U + 2 * E]).then_inc(s_rowsT, 1)
            for m in range(0, lead(0), 2):
                first_score_max(m)
            pe.wait_ge(s_cols, 1)
            turn_qr(0, 0)
            def down(b, w):
                e, c = w // HC, w % HC
                v = b * U + w
                pe.wait_ge(hh_done, v + 1)
                if c == 0 and e >= 2:
                    pe.wait_ge(comb_done, E * b + e - 1)
                ws = slice(P * w, P * w + P)
                pe.matmul(Y[e % 2], wh[:, 1, ws], hh[:, w % RING, :], start=(c == 0), stop=False)
                pe.matmul(Y[e % 2], wl[:, 1, ws], hh[:, w % RING, :], start=False, stop=False)
                pe.wait_ge(hl_done, v + 1)
                pe.matmul(Y[e % 2], wh[:, 1, ws], hl[:, w % RING, :], start=False, stop=(c == HC - 1)).then_inc(down_done, 1)

            for b in range(B):
                nxt = b + 1 < B
                for s in range(SLOTS):
                    sm = sm_of_slot(b, s)
                    for m in sm[0:1]:
                        score_max(b, m)
                    if nxt and s == SLOTS - 1:
                        turn_k(b + 1, 0)
                    for g in range(G):
                        if s == ot_slot(g):
                            turn_out(b, g)
                    if s < 4 * G:
                        score_pair(b, s, 0)
                    for m in sm[1:2]:
                        score_max(b, m)
                    if s < 4 * G:
                        score_pair(b, s, 1)
                    for m in sm[2:3]:
                        score_max(b, m)
                    for m in sm[3:4]:
                        score_max(b, m)
                    if s in QR:
                        turn_qr(b, QR.index(s))
                    if nxt and s == 15:
                        project(b + 1, 2)
                        project(b + 1, 3)
                    if 1 <= s <= 4 * G:
                        values(b, s - 1)
                    for m in sm[4:]:
                        score_max(b, m)
                    if nxt and s == 13:
                        turn_x(b + 1)
                    if nxt and s == 14:
                        project(b + 1, 0)
                        project(b + 1, 1)
                if b >= 1:
                    for w in range(U - DEFER, U - DEFER + 3):
                        down(b - 1, w)
                if nxt:
                    turn_k(b + 1, 1)
                if b >= 1:
                    for w in range(U - DEFER + 3, U - 3):
                        down(b - 1, w)
                if nxt:
                    turn_q(b + 1, 0)
                for t in range(T):
                    pe.wait_ge(ln_done[1], T * b + t + 1)
                    last = pe.transpose(MISC[:, P * t:P * t + P], xn[:, 1, t, :], ident[:, :])
                last.then_inc(x2_full, 1)
                if nxt:
                    turn_q(b + 1, 1)
                pe.wait_ge(x2_done, 2 * b + 1)
                for t in range(T):
                    last = pe.matmul(AV[:, E * t:E * t + E], x2f[:, P * t:P * t + P], cols[:, U:U + E],
                                     start=True, stop=True)
                last.then_inc(lg_full, 1)
                if b == 0:
                    pe.wait_ge(s_wl, W_CHUNKS)
                for u in range(steps(b)):
                    if u < U:
                        v = b * U + u
                        if u == 0:
                            pe.wait_ge(x2_done, 2 * (b + 1))
                        if u >= 2:
                            pe.wait_ge(gelu_done, v - 1)
                        w = slice(P * u, P * u + P)
                        pe.matmul(UP[u % 2], wh[:, 0, w], x2h[:, :], start=True, stop=False)
                        pe.matmul(UP[u % 2], wl[:, 0, w], x2h[:, :], start=False, stop=False)
                        if u == 0:
                            pe.wait_ge(x2l_done, b + 1)
                        pe.matmul(UP[u % 2], wh[:, 0, w], x2l[:, :], start=False, stop=True).then_inc(up_full, 1)
                    if u == 7:
                        pe.wait_ge(cw_done, b + 1)
                        if b >= 1:
                            pe.wait_ge(res_done, b)
                        for t in range(T):
                            last = pe.transpose(MISC16[0:2 * E, P * t:P * t + P],
                                                cwhl[:, t, :, :].rearrange("p a e -> p (a e)"), ident16[:, :])
                        last.then_inc(cwT_full, 1)
                    e = u - 8
                    if 0 <= e < E:
                        if e == 0:
                            pe.wait_ge(cwT_done, b + 1)
                        else:
                            pe.wait_ge(cwb_done, E * b + e)
                        pe.matmul(MISC[:, :], pick[:, e, :], cwT[:, :], start=True, stop=True).then_inc(cwb_full, 1)
                    if b >= 1 and u == 1:
                        for w in range(U - 3, U):
                            down(b - 1, w)
                    if b >= 1 and u == 5:
                        turn_sum(b - 1)
                    sm = sm_of_unit(u) if nxt else []
                    for m in sm[0:1]:
                        score_max(b + 1, m)
                    if nxt and u == U - 4:
                        turn_qr(b + 1, 0)
                    if 0 <= u - LAG_DN < units_down(b):
                        down(b, u - LAG_DN)
                    for m in sm[1:]:
                        score_max(b + 1, m)
            turn_sum(B - 1)


_INS = ["L0_attn_x", "L0_attn_Wq", "L0_attn_bq", "L0_attn_Wk", "L0_attn_bk",
        "L0_ffn_w_gate", "L0_ffn_W1", "L0_ffn_b1", "L0_ffn_W2", "L0_ffn_b2"]


def kernel(**inputs):
    import concourse.bacc as bacc
    from concourse.bass_utils import run_bass_kernel_spmd

    nc = bacc.Bacc("TRN2", target_bir_lowering=False, num_devices=1)
    arrays, args = {}, []
    for name in _INS:
        a = np.ascontiguousarray(inputs[name])
        arrays[name] = a
        args.append(nc.dram_tensor(name, a.shape, mybir.dt.from_np(a.dtype), kind="ExternalInput").ap())
    args.append(nc.dram_tensor("out", inputs["L0_attn_x"].shape, F32, kind="ExternalOutput").ap())
    preln_attention_moe(nc, *args)
    r = run_bass_kernel_spmd(nc, [arrays], core_ids=[0])
    return r.results[0]["out"]
```
